# Optimizing a Trainium2 kernel written in Bass

```python
import numpy as np
import jax
import jax.numpy as jnp

def _softmax(x, axis=-1):
    return jax.nn.softmax(x, axis=axis)

def _gelu(x):
    return jax.nn.gelu(x, approximate=True)

def _silu(x):
    return jax.nn.silu(x)

def _sigmoid(x):
    return jax.nn.sigmoid(x)

def _layernorm(x, axis=-1, eps=1e-05):
    m = jnp.mean(x, axis=axis, keepdims=True)
    v = jnp.var(x, axis=axis, keepdims=True)
    return (x - m) / jnp.sqrt(v + eps)

def _scatter_add(tgt, idx, src, axis=0):
    return tgt.at[idx].add(src)

def _segment_sum(src, seg, n):
    return jax.ops.segment_sum(src, seg, n)
kernel_name = 'mk_audio_tower_d1_tok_audfeat256_r4_a5d4a3'

def setup_inputs(seed: int=0):
    np.random.seed(seed)
    _w = jnp.asarray

    def _rec_inputs():
        import jax
        import jax.numpy as jnp
        _rk = jax.random.key(seed)
        x = -0.000520686 + 1.00062 * jax.random.normal(jax.random.fold_in(_rk, 1), (64, 750, 64), jnp.float32)
        return x
    x = _rec_inputs()

    def _L0_tok_setup():
        import jax, jax.numpy as jnp
        import numpy as np
        BATCH = 2
        SEQ = 1024
        D_MODEL = 64
        N_STATE = 64
        DT_RANK = 1
        NUM_LAYERS = 3

        def _ssm_layer(x, A_log, Dp, W_dbc, W_dt, b_dt):
            A = -jnp.exp(A_log)
            dbc = jnp.einsum('ble,ce->blc', x, W_dbc)
            delta, Bm, Cm = jnp.split(dbc, [DT_RANK, DT_RANK + N_STATE], axis=-1)
            delta = jax.nn.softplus(jnp.einsum('blr,er->ble', delta, W_dt) + b_dt)
            dA = jnp.exp(delta[..., None] * A)
            dBx = (delta * x)[..., None] * Bm[:, :, None, :]

            def combine(c1, c2):
                a1, h1 = c1
                a2, h2 = c2
                return (a1 * a2, h1 * a2 + h2)
            _, hs = jax.lax.associative_scan(combine, (dA, dBx), axis=1)
            y = jnp.einsum('blen,bln->ble', hs, Cm)
            return y + Dp * x
        key = jax.random.key(seed)
        kx, kw1, kw2 = jax.random.split(key, 3)
        x = jax.random.normal(kx, (BATCH, SEQ, D_MODEL), dtype=jnp.float32)
        A_log = jnp.broadcast_to(jnp.log(jnp.arange(1, N_STATE + 1, dtype=jnp.float32)), (NUM_LAYERS, D_MODEL, N_STATE)).copy()
        D = jnp.ones((NUM_LAYERS, D_MODEL), dtype=jnp.float32)
        W_dbc = 0.02 * jax.random.normal(kw1, (NUM_LAYERS, DT_RANK + 2 * N_STATE, D_MODEL), dtype=jnp.float32)
        W_dt = 0.02 * jax.random.normal(kw2, (NUM_LAYERS, D_MODEL, DT_RANK), dtype=jnp.float32)
        b_dt = jnp.zeros((NUM_LAYERS, D_MODEL), dtype=jnp.float32)
        return {'x': x, 'A_log': A_log, 'D': D, 'W_dbc': W_dbc, 'W_dt': W_dt, 'b_dt': b_dt}
    _L0_tok_all = _L0_tok_setup()
    _L0_tok_in = {k: v for k, v in _L0_tok_all.items() if k in ('A_log', 'D', 'W_dbc', 'W_dt', 'b_dt')}
    del _L0_tok_all

    def _L0_attn_setup():
        import jax, jax.numpy as jnp
        from jax import lax
        import numpy as np
        D_MODEL = 64
        EXPAND = 2
        D_INNER = D_MODEL * EXPAND
        B, T = (8, 1024)
        key = jax.random.key(seed)
        ks = jax.random.split(key, 7)
        s_lin = 1.0 / np.sqrt(D_MODEL)
        s_gru_i = 1.0 / np.sqrt(D_MODEL)
        x = jax.random.normal(ks[0], (B, T, D_MODEL), dtype=jnp.float32)
        W1 = jax.random.uniform(ks[1], (D_INNER, D_MODEL), jnp.float32, -s_lin, s_lin)
        b1 = jax.random.uniform(ks[2], (D_INNER,), jnp.float32, -s_lin, s_lin)
        W_ih = jax.random.uniform(ks[3], (3 * D_MODEL, D_INNER), jnp.float32, -s_gru_i, s_gru_i)
        b_ih = jax.random.uniform(ks[4], (3 * D_MODEL,), jnp.float32, -s_gru_i, s_gru_i)
        W_hh = jax.random.uniform(ks[5], (3 * D_MODEL, D_MODEL), jnp.float32, -s_gru_i, s_gru_i)
        b_hh = jax.random.uniform(ks[6], (3 * D_MODEL,), jnp.float32, -s_gru_i, s_gru_i)
        return {'x': x, 'W1': W1, 'b1': b1, 'W_ih': W_ih, 'b_ih': b_ih, 'W_hh': W_hh, 'b_hh': b_hh}
    _L0_attn_all = _L0_attn_setup()
    _L0_attn_in = {k: v for k, v in _L0_attn_all.items() if k in ('W1', 'b1', 'W_ih', 'b_ih', 'W_hh', 'b_hh')}
    del _L0_attn_all

    def _L0_ffn_setup():
        import jax, jax.numpy as jnp
        import numpy as np
        NUM_EXPERTS = 8
        TOP_K = 2
        B, S, D = (8, 2048, 64)

        def _moe(tokens, router_w, w1, b1, w2, b2):
            N = tokens.shape[0]
            E = router_w.shape[0]
            logits = tokens.astype(jnp.float32) @ router_w.astype(jnp.float32).T
            probs = jax.nn.softmax(logits, axis=-1)
            rw, re = jax.lax.top_k(probs, TOP_K)
            if TOP_K > 1:
                rw = rw / jnp.maximum(rw.sum(-1, keepdims=True), 1e-12)
            rw = rw.astype(tokens.dtype)
            combine = jnp.zeros((N, E), tokens.dtype).at[jnp.arange(N)[:, None], re].set(rw)
            out = tokens
            for e in range(E):
                h = jax.nn.gelu(tokens @ w1[e] + b1[e], approximate=False)
                y = h @ w2[e] + b2[e]
                out = out + combine[:, e:e + 1] * y
            return out
        key = jax.random.key(seed)
        ks = jax.random.split(key, 4)
        scale = 1.0 / np.sqrt(D).astype(np.float32)
        return {'input_embeddings': jax.random.normal(ks[0], (B, S, D), jnp.float32), 'router_w': jax.random.normal(ks[1], (NUM_EXPERTS, D), jnp.float32) * scale, 'w1': jax.random.normal(ks[2], (NUM_EXPERTS, D, D), jnp.float32) * scale, 'b1': jnp.zeros((NUM_EXPERTS, D), jnp.float32), 'w2': jax.random.normal(ks[3], (NUM_EXPERTS, D, D), jnp.float32) * scale, 'b2': jnp.zeros((NUM_EXPERTS, D), jnp.float32)}
    _L0_ffn_all = _L0_ffn_setup()
    _L0_ffn_in = {k: v for k, v in _L0_ffn_all.items() if k in ('router_w', 'w1', 'b1', 'w2', 'b2')}
    del _L0_ffn_all
    return {'x': x, 'L0_tok_A_log': _L0_tok_in['A_log'], 'L0_tok_D': _L0_tok_in['D'], 'L0_tok_W_dbc': _L0_tok_in['W_dbc'], 'L0_tok_W_dt': _L0_tok_in['W_dt'], 'L0_tok_b_dt': _L0_tok_in['b_dt'], 'L0_attn_W1': _L0_attn_in['W1'], 'L0_attn_b1': _L0_attn_in['b1'], 'L0_attn_W_ih': _L0_attn_in['W_ih'], 'L0_attn_b_ih': _L0_attn_in['b_ih'], 'L0_attn_W_hh': _L0_attn_in['W_hh'], 'L0_attn_b_hh': _L0_attn_in['b_hh'], 'L0_ffn_router_w': _L0_ffn_in['router_w'], 'L0_ffn_w1': _L0_ffn_in['w1'], 'L0_ffn_b1': _L0_ffn_in['b1'], 'L0_ffn_w2': _L0_ffn_in['w2'], 'L0_ffn_b2': _L0_ffn_in['b2']}

def reference(x, L0_tok_A_log, L0_tok_D, L0_tok_W_dbc, L0_tok_W_dt, L0_tok_b_dt, L0_attn_W1, L0_attn_b1, L0_attn_W_ih, L0_attn_b_ih, L0_attn_W_hh, L0_attn_b_hh, L0_ffn_router_w, L0_ffn_w1, L0_ffn_b1, L0_ffn_w2, L0_ffn_b2):
    import jax
    import jax.numpy as jnp

    def _L0_tok_ref(x, A_log, D, W_dbc, W_dt, b_dt):
        import jax, jax.numpy as jnp
        import numpy as np
        BATCH = 2
        SEQ = 1024
        D_MODEL = 64
        N_STATE = 64
        DT_RANK = 1
        NUM_LAYERS = 3

        def _ssm_layer(x, A_log, Dp, W_dbc, W_dt, b_dt):
            A = -jnp.exp(A_log)
            dbc = jnp.einsum('ble,ce->blc', x, W_dbc)
            delta, Bm, Cm = jnp.split(dbc, [DT_RANK, DT_RANK + N_STATE], axis=-1)
            delta = jax.nn.softplus(jnp.einsum('blr,er->ble', delta, W_dt) + b_dt)
            dA = jnp.exp(delta[..., None] * A)
            dBx = (delta * x)[..., None] * Bm[:, :, None, :]

            def combine(c1, c2):
                a1, h1 = c1
                a2, h2 = c2
                return (a1 * a2, h1 * a2 + h2)
            _, hs = jax.lax.associative_scan(combine, (dA, dBx), axis=1)
            y = jnp.einsum('blen,bln->ble', hs, Cm)
            return y + Dp * x
        for i in range(NUM_LAYERS):
            x = _ssm_layer(x, A_log[i], D[i], W_dbc[i], W_dt[i], b_dt[i])
            if i < NUM_LAYERS - 1:
                b, l, d = x.shape
                x = x[:, :l // 2 * 2].reshape(b, l // 2, 2, d).mean(axis=2)
        return x

    def _L0_attn_ref(x, W1, b1, W_ih, b_ih, W_hh, b_hh):
        import jax, jax.numpy as jnp
        from jax import lax
        import numpy as np
        D_MODEL = 64
        EXPAND = 2
        D_INNER = D_MODEL * EXPAND
        B, T = (8, 1024)
        h = jax.nn.gelu(jnp.einsum('btd,id->bti', x, W1) + b1, approximate=False)
        Bb, Tt, _ = h.shape
        H = W_hh.shape[1]
        gx = jnp.einsum('bti,gi->btg', h, W_ih) + b_ih
        gx = jnp.moveaxis(gx, 1, 0)

        def step(hprev, g):
            gh = hprev @ W_hh.T + b_hh
            xr, xz, xn = jnp.split(g, 3, axis=-1)
            hr, hz, hn = jnp.split(gh, 3, axis=-1)
            r = jax.nn.sigmoid(xr + hr)
            z = jax.nn.sigmoid(xz + hz)
            n = jnp.tanh(xn + r * hn)
            hnew = (1.0 - z) * n + z * hprev
            return (hnew, hnew)
        h0 = jnp.zeros((Bb, H), dtype=x.dtype)
        _, out = lax.scan(step, h0, gx)
        return jnp.moveaxis(out, 0, 1)

    def _L0_ffn_ref(input_embeddings, router_w, w1, b1, w2, b2):
        import jax, jax.numpy as jnp
        import numpy as np
        NUM_EXPERTS = 8
        TOP_K = 2
        B, S, D = (8, 2048, 64)

        def _moe(tokens, router_w, w1, b1, w2, b2):
            N = tokens.shape[0]
            E = router_w.shape[0]
            logits = tokens.astype(jnp.float32) @ router_w.astype(jnp.float32).T
            probs = jax.nn.softmax(logits, axis=-1)
            rw, re = jax.lax.top_k(probs, TOP_K)
            if TOP_K > 1:
                rw = rw / jnp.maximum(rw.sum(-1, keepdims=True), 1e-12)
            rw = rw.astype(tokens.dtype)
            combine = jnp.zeros((N, E), tokens.dtype).at[jnp.arange(N)[:, None], re].set(rw)
            out = tokens
            for e in range(E):
                h = jax.nn.gelu(tokens @ w1[e] + b1[e], approximate=False)
                y = h @ w2[e] + b2[e]
                out = out + combine[:, e:e + 1] * y
            return out
        b, s, d = input_embeddings.shape
        tokens = input_embeddings.reshape(b * s, d)
        return _moe(tokens, router_w, w1, b1, w2, b2).reshape(b, s, d)
    h = _L0_tok_ref(x, L0_tok_A_log, L0_tok_D, L0_tok_W_dbc, L0_tok_W_dt, L0_tok_b_dt)
    h = h + _L0_attn_ref(_layernorm(h, axis=-1), L0_attn_W1, L0_attn_b1, L0_attn_W_ih, L0_attn_b_ih, L0_attn_W_hh, L0_attn_b_hh)
    h = h + _L0_ffn_ref(_layernorm(h, axis=-1), L0_ffn_router_w, L0_ffn_w1, L0_ffn_b1, L0_ffn_w2, L0_ffn_b2)
    return h

_drawn_inputs = setup_inputs


def setup_inputs(seed=0):
    import zlib

    import numpy as np

    out = dict(_drawn_inputs(seed))
    spreads = {'L0_tok_D': (1.0, 0.2),
     'L0_tok_b_dt': (0.0, 0.346),
     'L0_ffn_b1': (0.0, 0.1),
     'L0_ffn_b2': (0.0, 0.1)}
    factors = {'L0_tok_A_log': 2.833, 'L0_tok_W_dt': 37.608}
    for name, (base, spread) in spreads.items():
        noise = np.random.default_rng([zlib.crc32(name.encode()), seed]).standard_normal(out[name].shape)
        drawn = base * np.exp(spread * noise) if base else spread * noise
        out[name] = jnp.asarray(drawn.astype(out[name].dtype))
    for name, factor in factors.items():
        out[name] = (out[name] * factor).astype(out[name].dtype)
    return out
```

```python
import concourse.bass as bass
from concourse import mybir
from contextlib import ExitStack

FP32 = mybir.dt.float32
BF16 = mybir.dt.bfloat16
ALU = mybir.AluOpType
ACT = mybir.ActivationFunctionType

HALF = 64
PAIRS = 32
T = 5
COLS = T * PAIRS
SEQ = [750, 375, 187]
CHUNKS = [-(-s // T) for s in SEQ]
FIRST = [0, CHUNKS[0], CHUNKS[0] + CHUNKS[1]]
TOTAL = sum(CHUNKS)
SLOTS = 2 * T
YROWS = 80
YT = 2 * COLS // YROWS
STEPS = HALF // 2
SPARE = slice(2 * COLS, 3 * COLS)
Z_STEP, B_STEP, C_STEP, P0_STEP, P1_STEP, TR_STEP = 2, 3, 1, 13, 17, 30
Y_STEPS = range(4, 31)


def layer_of(g):
    return 2 if g >= FIRST[2] else 1 if g >= FIRST[1] else 0


def build(nc, io, stop=None):
    ctx = ExitStack()
    with ctx:
        def sb(name, shape, dt=FP32):
            return ctx.enter_context(nc.sbuf_tensor(name, shape, dt))

        def ps(name, shape):
            return ctx.enter_context(nc.psum_tensor(name, shape, FP32))

        def sem(name):
            return ctx.enter_context(nc.semaphore(name))

        xT, AlogT, Dp, WT, Wr, Wdt, bdt, sel_d, id_d = (io[k] for k in ("xT", "AlogT", "D", "WT", "Wr", "Wdt", "bdt", "sel", "ident"))
        y_dram = [nc.dram_tensor(f"y{i}", [CHUNKS[i] * T, PAIRS, 128], FP32, kind="Internal").ap() for i in range(2)]
        y_dram.append(io["y2"])
        x_dram = [xT, nc.dram_tensor("x1", [CHUNKS[1], 128, COLS], FP32, kind="Internal").ap(), io["x2"]]

        hb = [sb(f"h{k}", [128, HALF, T, PAIRS]) for k in range(3)]
        row = [sb(f"row{k}", [128, 16, 2, COLS], BF16) for k in range(3)]
        cz = [sb(f"cz{k}", [128, PAIRS, 32]) for k in range(3)]
        xin = [sb(f"xin{k}", [128, COLS]) for k in range(3)]
        bt = [sb(f"bt{k}", [128, COLS]) for k in range(3)]
        zt = sb("zt", [128, COLS])
        rz = sb("rz", [128, COLS])
        dd = sb("dd", [128, 2, COLS])
        d3 = sb("d3", [128, 3, 2, COLS], BF16)
        ysb = sb("ysb", [128, 8, T * HALF])
        yld = sb("yld", [YROWS, YT, 128])
        xprev = sb("xprev", [128, 2, COLS])
        wbd = sb("wbd", [128, 3, 3, 128])
        wr = sb("wr", [128, 3])
        at = sb("at", [128, 3, HALF])
        dsk = sb("dsk", [128, 3])
        wdt = sb("wdt", [128, 3])
        bd = sb("bd", [128, 3])
        sel = sb("sel", [128, 128], BF16)
        ident = sb("ident", [128, 128])
        psX = ps("psX", [128, 2, 32, PAIRS])
        psD = [ps(f"psD{k}", [128, 512]) for k in range(2)]
        psC = [ps(f"psC{k}", [128, 512]) for k in range(2)]

        S = {n: sem(n) for n in (
            "s_const s_wz s_wd s_wrep s_ea s_at s_xt0 s_xt1 s_xt2 s_yl s_xp s_tr s_xo s_xs s_xin s_x1s s_rb s_za s_rz s_zl s_bt s_dl s_dd s_p0 "
            "s_r1 s_bb s_p1 s_p2 s_row0 s_row1 s_row2 s_cp s_cz s_db s_exp s_dxb s_m s_u s_h s_c s_ev s_y0 s_y1 s_psz").split()}
        s_row = [S["s_row0"], S["s_row1"], S["s_row2"]]
        s_xt = [S["s_xt0"], S["s_xt1"], S["s_xt2"]]
        s_y = [S["s_y0"], S["s_y1"]]
        block = ctx.enter_context(nc.Block())
        N_CONST = 10

        turn = [0]
        def plan():
            out = [("one", p) for p in (-3, -2, -1, 0, 1)]
            for l in range(3):
                a, b = FIRST[l] + 2, FIRST[l] + CHUNKS[l] - 4
                if l == 2:
                    b -= 1
                n = (b - a + 1) // 3
                out.append(("loop", a, n))
                nxt = FIRST[l + 1] + 2 if l < 2 else TOTAL + 2
                out += [("one", p) for p in range(a + 3 * n, nxt)]
            return out

        def run(eng, period):
            def layers(p):
                return [layer_of(g) if 0 <= g < TOTAL else None for g in range(p - 1, p + 4)]
            for item in plan():
                if item[0] == "one":
                    p = item[1]
                    turn[0] = 0
                    period(p, p % 3, layers(p), p)
                else:
                    _, a, n = item
                    with eng.Fori(0, n) as i:
                        turn[0] = i
                        for j in range(3):
                            period(i * 3 + (a + j), (a + j) % 3, layers(a + j), a + j)

        def wait(eng, s, value, least):
            if least > 0:
                eng.wait_ge(s, value)

        def snap(eng, v):
            return v if isinstance(v, int) else eng.snap(v)

        def thirds(c, c0):
            return turn[0] + (c0 // 3 + 1)

        def y_step(i):
            return Y_STEPS[i * len(Y_STEPS) // PAIRS]

        @block.sync
        def _(sp):
            for b in range(2):
                h = slice(b * 64, b * 64 + 64)
                sp.dma_start(at[h, :, :], AlogT.rearrange("l n e -> n l e")).then_inc(S["s_const"], 16)
                sp.dma_start(wr[h, :], Wr).then_inc(S["s_const"], 16)
                sp.dma_start(dsk[h, :], Dp).then_inc(S["s_const"], 16)
                sp.dma_start(wdt[h, :], Wdt).then_inc(S["s_const"], 16)
                sp.dma_start(bd[h, :], bdt).then_inc(S["s_const"], 16)
            sp.dma_start(sel[:], sel_d).then_inc(S["s_const"], 16)
            sp.dma_start(ident[:], id_d).then_inc(S["s_const"], 16)
            sp.wait_ge(S["s_wz"], 1)
            for b in range(2):
                h = slice(b * 64, b * 64 + 64)
                for l in range(3):
                    sp.dma_start(wbd[h, l, 1:3, h], WT[l, :, 1:129].rearrange("k (v n) -> k v n", v=2)).then_inc(S["s_wd"], 16)

            def load_x(c, c0, k):
                at_c, used = snap(sp, c), snap(sp, c - 2)
                wait(sp, S["s_cp"], used, c0 - 2)
                wait(sp, S["s_dd"], used, c0 - 2)
                sp.dma_start(xin[k][:], xT[bass.ds(at_c, 1), :, :].rearrange("c p n -> (c p) n")).then_inc(s_xt[k], 16)

            def load_y(c, c0, l):
                n, n0 = c - FIRST[l], c0 - FIRST[l]
                chunks = min(2, CHUNKS[l - 1] - 2 * n0)
                at_row, at_x = snap(sp, n * (2 * COLS)), snap(sp, n * 2)
                stored = snap(sp, (n * 2 + (FIRST[l - 1] + chunks)) * 80)
                x_stored = snap(sp, (n * 2 + chunks) * 16)
                used = snap(sp, c - FIRST[1])
                wait(sp, S["s_xs"], used, c0 - FIRST[1])
                sp.wait_ge(s_y[0], stored)
                sp.wait_ge(s_y[1], stored)
                if l == 2:
                    sp.wait_ge(S["s_x1s"], x_stored)
                rows = y_dram[l - 1].rearrange("t p f -> (t p) f")
                sp.dma_start(yld[:, 0:chunks * YT // 2, :],
                             rows[bass.ds(at_row, chunks * COLS), :].rearrange("(i r) f -> r i f", r=YROWS)).then_inc(S["s_yl"], 16)
                sp.dma_start(xprev[:, 0:chunks, :],
                             x_dram[l - 1][bass.ds(at_x, chunks), :, :].rearrange("c p n -> p c n")).then_inc(S["s_xp"], 16)

            def store_x(c, c0, l):
                at_c, there = snap(sp, c - FIRST[l]), snap(sp, c - (FIRST[1] - 1))
                sp.wait_ge(S["s_xin"], there)
                sp.dma_start(x_dram[l][bass.ds(at_c, 1), :, :].rearrange("c p n -> (c p) n"), xin[c0 % 3][:]).then_inc(S["s_x1s"], 16)

            def rows_out(c, c0):
                k = c0 % 3
                sp.wait_ge(S["s_p2"], c + 1)
                for b in range(2):
                    for s in range(3):
                        sp.dma_start(row[k][3 * b + s:128:32, :, :, :],
                                     d3[b * 64:b * 64 + 64, s, :, :]).then_inc(s_row[k], 16)

            def store_y(c, c0, half, l):
                at_t, there = [snap(sp, (c - FIRST[l]) * T + t) for t in range(T)], snap(sp, c * 8 + (4 * half + 4))
                sp.wait_ge(S["s_ev"], there)
                for t in range(T):
                    dst = y_dram[l][bass.ds(at_t[t], 1), 16 * half:16 * half + 16, :]
                    sp.dma_start(dst.rearrange("t (g j) (b e) -> (j t b) g e", j=4, b=2),
                                 ysb[t:128:16, 4 * half:4 * half + 4, t * HALF:(t + 1) * HALF]).then_inc(s_y[half], 16)

            def period(p, k, ls, p0):
                if 2 <= p0:
                    store_y(p - 2, p0 - 2, 1, layer_of(p0 - 2))
                c, c0 = p + 2, p0 + 2
                l = ls[3]
                if ls[4] == 0:
                    load_x(p + 3, p0 + 3, (p0 + 3) % 3)
                if ls[4]:
                    load_y(p + 3, p0 + 3, ls[4])
                if l is not None and l > 0:
                    store_x(c, c0, l)
                if l is not None:
                    rows_out(c, c0)
                if ls[0] is not None:
                    store_y(p - 1, p0 - 1, 0, ls[0])

            run(sp, period)
            for h in range(2):
                sp.wait_ge(s_y[h], 80 * TOTAL)
            sp.wait_ge(S["s_x1s"], 16 * (CHUNKS[1] + CHUNKS[2]))

        @block.gpsimd
        def _(pool):
            nc.gpsimd.memset(wbd[:], 0.0).then_inc(S["s_wz"], 1)
            for k in range(3):
                nc.gpsimd.memset(cz[k][:], 0.0).then_inc(S["s_psz"], 1)

            def period(p, k, ls, p0):
                l = ls[1]
                if l is None:
                    return
                for s in range(SLOTS):
                    t, es = s // 2, slice(32 * (s % 2), 32 * (s % 2) + 32)
                    now = hb[k][:, es, t, :]
                    if t == 0:
                        pool.wait_ge(S["s_exp"], p * 64 + 32 * (s + 1))
                        before = hb[(k + 2) % 3][:, es, T - 1, :]
                    else:
                        before = hb[k][:, es, t - 1, :]
                    if t == 0 and p0 in FIRST:
                        nc.gpsimd.memset(now, 0.0).then_inc(S["s_u"], 1)
                    else:
                        wait(pool, S["s_h"], p * SLOTS + (s - 1), p0 * SLOTS + s - 1)
                        nc.gpsimd.tensor_tensor(now, now, before, ALU.mult).then_inc(S["s_u"], 1)

            run(pool, period)

        @block.vector
        def _(dve):
            dve.wait_ge(S["s_const"], 16 * 12)
            dve.wait_ge(S["s_wz"], 1)
            for b in range(2):
                h = slice(b * 64, b * 64 + 64)
                for l in range(3):
                    nc.vector.tensor_copy(wbd[h, l, 0, h], wr[h, l:l + 1].broadcast_to([64, 64])).then_inc(S["s_wrep"], 1)
            dve.wait_ge(S["s_ea"], 1)
            nc.vector.tensor_scalar(at[:], at[:], -1.0, None, ALU.mult).then_inc(S["s_at"], 1)

            def period(p, k, ls, p0):
                c, c0, l2 = p + 2, p0 + 2, ls[3]
                kx = c0 % 3
                for s in range(SLOTS):
                    t, es = s // 2, slice(32 * (s % 2), 32 * (s % 2) + 32)
                    if ls[1] is not None:
                        n = p * SLOTS + (s + 1)
                        dve.wait_ge(S["s_dxb"], n)
                        if s == 0:
                            dve.wait_ge(S["s_bt"], p + 1)
                        b_t = bt[k][:, t * PAIRS:(t + 1) * PAIRS].unsqueeze(1).broadcast_to([128, 32, PAIRS])
                        nc.vector.tensor_tensor(psX[:, s % 2], psX[:, s % 2], b_t, ALU.mult).then_inc(S["s_m"], 1)
                        now = hb[k][:, es, t, :]
                        dve.wait_ge(S["s_m"], n)
                        dve.wait_ge(S["s_u"], n)
                        nc.vector.tensor_tensor(now, now, psX[:, s % 2], ALU.add).then_inc(S["s_h"], 1)
                    if s == 9 and ls[4]:
                        l4, n4, c4 = ls[4], p + (3 - FIRST[1]), p0 + 3 - FIRST[1]
                        dve.wait_ge(S["s_tr"], n4 + 1)
                        dve.wait_ge(S["s_xp"], (n4 + 1) * 16)
                        nc.vector.scalar_tensor_tensor(xprev[:].rearrange("p v n -> p (v n)"), xprev[:].rearrange("p v n -> p (v n)"), dsk[:, l4 - 1:l4],
                                                       psC[0][:, 0:2 * COLS], ALU.mult, ALU.add).then_inc(S["s_xo"], 1)
                        dve.wait_ge(S["s_xo"], n4 + 1)
                        dve.wait_ge(S["s_cp"], p + 1)
                        wait(dve, S["s_x1s"], (n4 - 2) * 16, (c4 - 2) * 16)
                        pairs = xprev[:].rearrange("p v (t n) -> p (v t) n", t=T)
                        nc.vector.tensor_tensor(xin[k][:].rearrange("p (t n) -> p t n", t=T), pairs[:, 0:2 * T:2, :], pairs[:, 1:2 * T:2, :],
                                                ALU.add).then_inc(S["s_xs"], 1)
                    if l2 is None:
                        continue
                    if s == 3:
                        dve.wait_ge(S["s_zl"], c + 1)
                        dve.wait_ge(S["s_rz"], c + 1)
                        wait(dve, S["s_p2"], c, c0)
                        nc.vector.tensor_tensor(dd[:, 0, :], zt[:], rz[:], ALU.add).then_inc(S["s_dl"], 1)
                        dve.wait_ge(S["s_dl"], c + 1)
                        nc.vector.tensor_tensor(dd[:, 1, :], dd[:, 0, :], xin[kx][:], ALU.mult).then_inc(S["s_dd"], 1)
                    if s == 4:
                        dve.wait_ge(S["s_p0"], c + 1)
                        nc.vector.tensor_tensor(dd[:], dd[:], d3[:, 0], ALU.subtract).then_inc(S["s_r1"], 1)
                    if s == 5:
                        dve.wait_ge(S["s_p1"], c + 1)
                        nc.vector.tensor_tensor(d3[:, 2], dd[:], d3[:, 1], ALU.subtract).then_inc(S["s_p2"], 1)

            run(dve, period)

        @block.scalar
        def _(act):
            act.preload_act_table_set("natural_log_exp_and_others")
            act.wait_ge(S["s_const"], 16 * 12)
            nc.scalar.activation(at[:], at[:], ACT.Exp).then_inc(S["s_ea"], 1)
            act.wait_ge(S["s_at"], 1)

            def period(p, k, ls, p0):
                c, c0, l2 = p + 2, p0 + 2, ls[3]
                kx = c0 % 3
                ke = (k + 1) % 3
                for i in range(STEPS):
                    if i == 0 and l2:
                        act.wait_ge(S["s_xs"], c - (FIRST[1] - 1))
                        nc.scalar.activation(xin[kx][:], xin[kx][:], ACT.Copy, scale=0.5).then_inc(S["s_xin"], 1)
                    if i == 0 and ls[2] is not None:
                        wait(act, S["s_c"], (p - 1) * 8, (p0 - 1) * 8)
                        wait(act, S["s_u"], (p - 1) * SLOTS + 2, (p0 - 1) * SLOTS + 2)
                    if i == Z_STEP and l2 is not None:
                        wait(act, S["s_dl"], c, c0)
                        act.wait_ge(S["s_rb"], c + 1)
                        z = psD[i % 2][:, SPARE]
                        nc.scalar.activation(zt[:], z, ACT.Abs, bias=bd[:, l2:l2 + 1], scale=wdt[:, l2:l2 + 1]).then_inc(S["s_za"], 1)
                        nc.scalar.activation(rz[:], z, ACT.Relu, bias=bd[:, l2:l2 + 1], scale=wdt[:, l2:l2 + 1]).then_inc(S["s_rz"], 1)
                    if i == B_STEP and l2 is not None:
                        act.wait_ge(S["s_za"], c * 2 + 1)
                        nc.scalar.activation(zt[:], zt[:], ACT.Exp, scale=-1.0).then_inc(S["s_za"], 1)
                        act.wait_ge(S["s_bb"], c + 1)
                        wait(act, S["s_m"], (c - 2) * SLOTS, (c0 - 2) * SLOTS)
                        nc.scalar.activation(bt[kx][:], psD[i % 2][:, SPARE], ACT.Copy).then_inc(S["s_bt"], 1)
                    if i == B_STEP + 1 and l2 is not None:
                        act.wait_ge(S["s_za"], c * 2 + 2)
                        nc.scalar.activation(zt[:], zt[:], ACT.Ln, bias=1.0).then_inc(S["s_zl"], 1)
                    if i == C_STEP and ls[1] is not None:
                        act.wait_ge(S["s_cp"], p + 1)
                        for b in range(2):
                            h = slice(b * 64, b * 64 + 64)
                            nc.scalar.activation(cz[k][h, :, 16 * b:16 * b + T], psD[i % 2][h, SPARE].rearrange("p (t n) -> p n t", t=T),
                                                 ACT.Copy).then_inc(S["s_cz"], 1)
                    if i == P0_STEP and l2 is not None:
                        act.wait_ge(S["s_dd"], c + 1)
                        if c0 > 0:
                            act.wait_ge(s_row[(c0 - 1) % 3], thirds(c - 1, c0 - 1) * 96)
                        nc.scalar.activation(d3[:, 0], dd[:], ACT.Copy).then_inc(S["s_p0"], 1)
                    if i == P1_STEP and l2 is not None:
                        act.wait_ge(S["s_r1"], c + 1)
                        nc.scalar.activation(d3[:, 1], dd[:], ACT.Copy).then_inc(S["s_p1"], 1)
                    if ls[2] is not None:
                        act.wait_ge(S["s_db"], (p + 1) * STEPS + (i + 1))
                        for e in (2 * i, 2 * i + 1):
                            nc.scalar.activation(hb[ke][:, e], psD[i % 2][:, (e % 2) * COLS:(e % 2 + 1) * COLS].rearrange("p (t n) -> p t n", t=T),
                                                 ACT.Exp, scale=at[:, ls[2], e:e + 1]).then_inc(S["s_exp"], 1)
                    for g in range(8):
                        if ls[0] is not None and i == min(y_step(4 * g + 3) + 2, STEPS - 1):
                            evac(p - 1, p0 - 1, g)

            def evac(c, c0, g):
                act.wait_ge(S["s_c"], c * 8 + (g + 1))
                if g % 4 == 0:
                    wait(act, s_y[g // 4], c * 80, c0)
                nc.scalar.activation(ysb[:, g, :], psC[g % 2][:, 0:T * HALF], ACT.Copy).then_inc(S["s_ev"], 1)

            run(act, period)

        @block.tensor
        def _(pe):
            pe.wait_ge(S["s_const"], 16 * 12)
            pe.wait_ge(S["s_wd"], 16 * 6)
            pe.wait_ge(S["s_wrep"], 6)
            pe.wait_ge(S["s_psz"], 3)

            def dx_broadcast(c, c0, k, s):
                t = s // 2
                wait(pe, S["s_h"], c * SLOTS + (s - 1), c0 * SLOTS + s - 1)
                for q in (0, 1):
                    e4 = 2 * (s % 2) + q
                    r = slice(32 * e4, 32 * e4 + 6)
                    last = nc.tensor.matmul(psX[:, s % 2, 16 * q:16 * q + 16, :], sel[r, :], row[k][r, :, 1, t * PAIRS:(t + 1) * PAIRS],
                                            start=True, stop=True)
                last.then_inc(S["s_dxb"], 1)

            def period(p, k, ls, p0):
                c, c0, l2 = p + 2, p0 + 2, ls[3]
                kx = c0 % 3
                ke = (k + 1) % 3
                if p0 == -1:
                    pe.wait_ge(S["s_rz"], 1)
                    pe.wait_ge(S["s_za"], 1)
                    pe.wait_ge(S["s_bt"], 1)
                for i in range(STEPS):
                    for s in range(SLOTS):
                        if i == STEPS * s // SLOTS + 1:
                            if s < SLOTS - 1 and ls[1] is not None:
                                dx_broadcast(p, p0, k, s + 1)
                            if s == SLOTS - 1 and ls[2] is not None:
                                dx_broadcast(p + 1, p0 + 1, ke, 0)
                    if ls[2] is not None:
                        if i == Z_STEP + 2 and l2 is not None:
                            pe.wait_ge(S["s_rz"], c + 1)
                            pe.wait_ge(S["s_za"], c * 2 + 1)
                        if i == B_STEP + 2 and l2 is not None:
                            pe.wait_ge(S["s_bt"], c + 1)
                        if i == C_STEP + 2 and ls[1] is not None:
                            pe.wait_ge(S["s_cz"], p * 2 + 2)
                        delta_broadcast(p + 1, p0 + 1, ke, i)
                    if i == Z_STEP and l2 is not None:
                        if l2 == 0:
                            pe.wait_ge(s_xt[kx], thirds(c, c0) * 16)
                        else:
                            pe.wait_ge(S["s_xin"], c - (FIRST[1] - 1))
                        nc.tensor.matmul(psD[i % 2][:, SPARE], wbd[:, l2, 0, :], xin[kx][:], start=True, stop=True).then_inc(S["s_rb"], 1)
                    if i == B_STEP and l2 is not None:
                        nc.tensor.matmul(psD[i % 2][:, SPARE], wbd[:, l2, 1, :], xin[kx][:], start=True, stop=True).then_inc(S["s_bb"], 1)
                    if i == C_STEP and ls[1] is not None:
                        if ls[2] is None:
                            pe.wait_ge(S["s_exp"], (p + 1) * HALF)
                        nc.tensor.matmul(psD[i % 2][:, SPARE], wbd[:, ls[1], 2, :], xin[k][:], start=True, stop=True).then_inc(S["s_cp"], 1)
                    if i == TR_STEP and ls[4]:
                        n4 = p + (3 - FIRST[1])
                        pe.wait_ge(S["s_yl"], (n4 + 1) * 16)
                        pe.wait_ge(S["s_ev"], (p - 1) * 8 + 7)
                        for j in range(YT):
                            last = nc.tensor.matmul(psC[0][:, j * YROWS:(j + 1) * YROWS], yld[:, j, :],
                                                    ident[0:YROWS, 0:YROWS], start=True, stop=True)
                        last.then_inc(S["s_tr"], 1)
                    if ls[0] is not None:
                        for j in range(PAIRS):
                            if y_step(j) == i:
                                y_matmul(p - 1, p0 - 1, (k + 2) % 3, j)

            def delta_broadcast(c, c0, k, ep):
                if ep == 0:
                    pe.wait_ge(s_row[k], thirds(c, c0) * 96)
                if c0 > 0 or ep >= 2:
                    pe.wait_ge(S["s_exp"], c * 64 + 2 * (ep - 1))
                r = slice(32 * (ep // 8), 32 * (ep // 8) + 6)
                nc.tensor.matmul(psD[ep % 2][:, 0:2 * COLS], sel[r, :], row[k][r, 2 * (ep % 8):2 * (ep % 8) + 2, 0, :],
                                 start=True, stop=True).then_inc(S["s_db"], 1)

            def y_matmul(c, c0, k, i):
                g, j = i // 4, i % 4
                if i == 0:
                    pe.wait_ge(S["s_h"], (c + 1) * SLOTS)
                    pe.wait_ge(S["s_cz"], (c + 1) * 2)
                if i == 0 and FIRST[1] - 3 <= c0 < TOTAL - 3:
                    pe.wait_ge(S["s_xo"], c + (4 - FIRST[1]))
                if j == 0 and (c0 > 0 or g >= 2):
                    pe.wait_ge(S["s_ev"], c * 8 + (g - 1))
                last = nc.tensor.matmul(psC[g % 2][32 * j:32 * j + 32, 0:T * HALF], cz[k][:, i, :], hb[k][:, :, :, i].rearrange("p e t -> p t e"),
                                        start=True, stop=True)
                if j == 3:
                    last.then_inc(S["s_c"], 1)

            run(pe, period)


GS = 11
GC = SEQ[2] // GS
GN = GS * PAIRS
NTOK = SEQ[2] * PAIRS
GROUP = 512
NG = -(-NTOK // GROUP)
TOK = NG * GROUP
TILES = GROUP // 128
E8 = 8
EPS = 1e-5


def tail(nc, io):
    ctx = ExitStack()
    with ctx:
        def sb(name, shape, dt=FP32):
            return ctx.enter_context(nc.sbuf_tensor(name, shape, dt))

        def ps(name, shape):
            return ctx.enter_context(nc.psum_tensor(name, shape, FP32))

        def sem(name):
            return ctx.enter_context(nc.semaphore(name))

        hT = sb("hT", [128, TOK])
        xT = sb("xnT", [128, TOK])
        yl = [sb(f"yl{k}", [128, TILES, 128]) for k in range(2)]
        sq = [sb(f"sq{k}", [128, GROUP]) for k in range(2)]
        sd = [sb(f"sd{k}", [128, GROUP]) for k in range(2)]
        hg = [sb(f"hg{b}", [128, GN]) for b in range(2)]
        gx = [sb(f"gx{k}", [128, GS, 4, PAIRS]) for k in range(2)]
        hs = [sb(f"hs{k}", [128, GS, PAIRS]) for k in range(2)]
        eps = sb("eps", [128, 1])
        one = sb("one", [128, 1])
        hcp = [sb(f"hcp{k}", [128, GROUP]) for k in range(2)]
        rzt = sb("rzt", [128, 2, PAIRS])
        nt = sb("nt", [128, PAIRS])
        nb = sb("nb", [128, PAIRS])
        zb = sb("zb", [128, PAIRS])
        za = sb("za", [128, PAIRS])
        w1t = sb("w1t", [128, 2, 128])
        b1 = sb("gb1", [128, 1])
        wih = sb("wih", [128, 192])
        whh = sb("whh", [128, 3, 128])
        bih = sb("bih", [128, 3])
        bhh = sb("bhh", [128, 3])
        ident = sb("tident", [128, 128])
        ones = sb("ones64", [128, 128])
        dsk = sb("tdsk", [128, 3])
        ew1 = sb("ew1", [128, 2, 4, 128])
        eb1 = sb("eb1", [128, 4])
        ew2 = sb("ew2", [128, 4, 128])
        eb2 = sb("eb2", [1, 512])
        one1 = sb("one1", [1, 128])
        rw = sb("rw", [128, 2, E8])
        down = sb("down", [128, E8])
        NT = NG * TILES * 2
        lg = sb("lg", [128, NT, E8])
        pr = sb("pr", [128, NT, E8])
        oh = sb("oh", [128, NT, E8])
        cb = sb("cb", [128, NT, E8])
        r1 = sb("r1v", [128, NT])
        r2 = sb("r2v", [128, NT])
        r3 = sb("r3v", [128, NT])
        he = [sb(f"he{k}", [128, 4, GROUP]) for k in range(2)]
        pd = [sb(f"pd{k}", [128, E8, HALF]) for k in range(2)]
        rd = [sb(f"rd{k}", [128, HALF]) for k in range(2)]
        ob = [sb(f"ob{k}", [128, TILES, 128]) for k in range(2)]
        bank = [ps(f"bank{k}", [128, 512]) for k in range(8)]

        names = ("t_c t_z t_w t_x t_y0 t_y1 t_tr t_h t_mean t_xc t_sq t_var t_sd t_rs t_xn t_h1 t_gel t_gxm t_gx t_pi t_pg t_rz t_rh t_rn t_nt t_zb "
                 "t_nb t_hs t_h4 t2_mean t2_xc t2_sq t2_var t2_sd t2_rs t2_xn t2_s t_rt t_cp t_lg t_q t_ex t_cb t_e1 t_eg t_ps t_pm t_rd t_rr t_ob t_o0 t_o1").split()
        S = {n: sem(n) for n in names}
        yrows = io["y2"].rearrange("t p f -> (t p) f")
        block = ctx.enter_context(nc.Block())
        NCONST = 24

        def run2(eng, n, body, start=0):
            if start == 0:
                body(0, 0, 0)
                body(1, 1, 1)
                start = 2
            with eng.Fori(start // 2, n // 2) as j:
                for u in range(2):
                    body(j * 2 + u, u, start + u)
            if n % 2:
                body(n - 1, 0, n - 1)

        def skewed(eng, n, first, second):
            first(0, 0, 0)

            def both(i, k, i0):
                first(i + 1, 1 - k, i0 + 1)
                second(i, k, i0)
            run2(eng, n - 1, both)
            second(n - 1, (n - 1) % 2, n - 1)

        def wait(eng, s, value, least):
            if least > 0:
                eng.wait_ge(S[s], value)

        def cols(i, n=GROUP, off=0):
            return bass.ds(i * n + off, n)

        @block.sync
        def _(sp):
            n = 0
            def load(dst, src):
                nonlocal n
                n += 1
                sp.dma_start(dst, src).then_inc(S["t_c"], 16)
            for b in range(2):
                h = slice(64 * b, 64 * b + 64)
                load(bih[h, :], io["bih"])
                load(bhh[h, :], io["bhh"])
                load(dsk[h, :], io["D"])
            load(b1[:], io["b1"])
            load(wih[:], io["WihT"])
            load(ident[:], io["ident"])
            load(ones[:], io["ones64"])
            load(eb1[:], io["eb1"])
            load(eb2[:], io["eb2"])
            load(one1[:], io["one1"])
            load(down[:], io["down"])
            load(hT[:, 0:CHUNKS[2] * COLS].rearrange("p (c n) -> p c n", n=COLS), io["x2"].rearrange("c p n -> p c n"))
            sp.wait_ge(S["t_z"], 8)
            for b in range(2):
                h = slice(64 * b, 64 * b + 64)
                load(whh[h, :, h], io["WhhT"].rearrange("j (g o) -> j g o", g=3))
                load(ew2[h, :, h], io["ew2"][b])
                load(w1t[h, b, :], io["W1T"])
                load(rw[h, b, :], io["rwT"])
                load(ew1[h, b, :, :], io["ew1"])
            assert n == 25, n
            def load_y(i, k, i0, rows=GROUP):
                at, used = (i * GROUP, i - 1) if isinstance(i, int) else (sp.snap(i * GROUP), sp.snap(i - 1))
                wait(sp, "t_tr", used, i0 - 1)
                full = rows // 128
                sp.dma_start(yl[k][:, 0:full, :], yrows[bass.ds(at, full * 128), :].rearrange("(k r) f -> r k f", r=128)).then_inc(S[f"t_y{k}"], 16)
                if rows % 128:
                    sp.dma_start(yl[k][0:rows % 128, full, :], yrows[i * GROUP + full * 128:i * GROUP + rows, :]).then_inc(S[f"t_y{k}"], 16)
            load_y(0, 0, 0)
            load_y(1, 1, 1)
            run2(sp, NG - 2, load_y, 2)
            load_y(NG - 2, 0, NG - 2)
            load_y(NG - 1, 1, NG - 1, CHUNKS[2] * COLS - (NG - 1) * GROUP)
            def out(i, k, i0):
                at = i * GROUP if isinstance(i, int) else sp.snap(i * GROUP)
                done = (i + 1) * (2 * TILES) if isinstance(i, int) else sp.snap((i + 1) * (2 * TILES))
                sp.wait_ge(S["t_ob"], done)
                sp.dma_start(io["out"][bass.ds(at, GROUP), :].rearrange("(k r) f -> r k f", r=128), ob[k][:]).then_inc(S[f"t_o{k}"], 16)
            run2(sp, NG, out)
            sp.wait_ge(S["t_o0"], 16 * (NG // 2))
            sp.wait_ge(S["t_o1"], 16 * (NG // 2))

        NC_ = 25 * 16

        @block.gpsimd
        def _(pool):
            nc.gpsimd.memset(whh[:], 0.0).then_inc(S["t_z"], 1)
            nc.gpsimd.memset(ew2[:], 0.0).then_inc(S["t_z"], 1)
            nc.gpsimd.memset(rw[:], 0.0).then_inc(S["t_z"], 1)
            nc.gpsimd.memset(w1t[:], 0.0).then_inc(S["t_z"], 1)
            nc.gpsimd.memset(ew1[:], 0.0).then_inc(S["t_z"], 1)
            nc.gpsimd.memset(hT[:, CHUNKS[2] * COLS:TOK], 0.0).then_inc(S["t_z"], 1)
            nc.gpsimd.memset(one[:], 1.0).then_inc(S["t_z"], 1)
            nc.gpsimd.memset(eps[:], EPS).then_inc(S["t_z"], 1)
            def copy(i, k, i0):
                pool.wait_ge(S["t2_s"], i + 1)
                wait(pool, "t_ps", (i - 1) * 8, i0 - 1)
                nc.gpsimd.tensor_copy(hcp[k][:], hT[:, cols(i)]).then_inc(S["t_cp"], 1)
            run2(pool, NG, copy)

        @block.vector
        def _(dve):
            dve.wait_ge(S["t_c"], NC_)
            dve.wait_ge(S["t_z"], 8)
            nc.vector.tensor_scalar(whh[:, 0:2], whh[:, 0:2], 0.5, None, ALU.mult).then_inc(S["t_w"], 1)
            nc.vector.tensor_scalar(whh[:, 2], whh[:, 2], 0.25, None, ALU.mult).then_inc(S["t_w"], 1)
            nc.vector.tensor_tensor(bih[:, 0:2], bih[:, 0:2], bhh[:, 0:2], ALU.add).then_inc(S["t_w"], 1)
            nc.vector.tensor_scalar(bhh[:, 2:3], bhh[:, 2:3], 0.5, None, ALU.mult).then_inc(S["t_w"], 1)
            dve.wait_ge(S["t_w"], 4)
            for k in range(2):
                nc.vector.tensor_copy(gx[k][:, :, 2, :], bhh[:, 2:3].unsqueeze(1).broadcast_to([128, GS, PAIRS])).then_inc(S["t_w"], 1)
            nc.vector.memset(hs[1][:, GS - 1, :], 0.0).then_inc(S["t_w"], 1)

            def center(pre):
                def body(i, k, i0):
                    if pre == "t":
                        dve.wait_ge(S["t_tr"], i + 1)
                        nc.vector.scalar_tensor_tensor(hT[:, cols(i)], hT[:, cols(i)], dsk[:, 2:3], bank[k][:],
                                                       ALU.mult, ALU.add).then_inc(S["t_h"], 1)
                    dve.wait_ge(S[pre + "_mean"], i + 1)
                    nc.vector.tensor_tensor(xT[:, cols(i)], hT[:, cols(i)], bank[2 + k][:], ALU.subtract).then_inc(S[pre + "_xc"], 1)
                return body

            def scale(pre):
                def body(i, k, i0):
                    dve.wait_ge(S[pre + "_sd"], i + 1)
                    nc.vector.reciprocal(sd[k][:], sd[k][:]).then_inc(S[pre + "_rs"], 1)
                    dve.wait_ge(S[pre + "_rs"], i + 1)
                    nc.vector.tensor_tensor(xT[:, cols(i)], xT[:, cols(i)], sd[k][:], ALU.mult).then_inc(S[pre + "_xn"], 1)
                    if pre == "t2":
                        dve.wait_ge(S[pre + "_xn"], i + 1)
                        nc.vector.tensor_tensor(hT[:, cols(i)], hT[:, cols(i)], xT[:, cols(i)], ALU.add).then_inc(S["t2_s"], 1)
                return body

            skewed(dve, NG, center("t"), scale("t"))

            def gru(i, k, i0):
                for s in range(GS):
                    m = i * GS + s
                    n_ps = bank[2 + (s + k) % 2]
                    before = hs[k][:, s - 1, :] if s else hs[1 - k][:, GS - 1, :]
                    dve.wait_ge(S["t_rz"], m + 1)
                    nc.vector.scalar_tensor_tensor(nt[:], rzt[:, 0], 1.0, n_ps[:, 64:96], ALU.add, ALU.mult).then_inc(S["t_rh"], 1)
                    dve.wait_ge(S["t_rh"], m + 1)
                    nc.vector.tensor_tensor(nt[:], nt[:], gx[k][:, s, 3, :], ALU.add).then_inc(S["t_rn"], 1)
                    wait(dve, "t_hs", m, i0 * GS + s)
                    nc.vector.scalar_tensor_tensor(za[:], rzt[:, 1], 1.0, before, ALU.add, ALU.mult).then_inc(S["t_q"], 1)
                    dve.wait_ge(S["t_nt"], m + 1)
                    dve.wait_ge(S["t_zb"], m + 1)
                    nc.vector.tensor_tensor(nb[:], nt[:], zb[:], ALU.mult).then_inc(S["t_nb"], 1)
                    dve.wait_ge(S["t_nb"], m + 1)
                    dve.wait_ge(S["t_q"], m + 1)
                    nc.vector.scalar_tensor_tensor(hs[k][:, s, :], za[:], 0.5, nb[:], ALU.mult, ALU.add).then_inc(S["t_hs"], 1)
                dve.wait_ge(S["t_hs"], (i + 1) * GS)
                nc.vector.scalar_tensor_tensor(hT[:, cols(i, GN)], hs[k][:].rearrange("p s n -> p (s n)"), 0.5, hT[:, cols(i, GN)],
                                               ALU.mult, ALU.add).then_inc(S["t_h4"], 1)

            run2(dve, GC, gru)
            dve.wait_ge(S["t_h4"], GC)
            skewed(dve, NG, center("t2"), scale("t2"))

            q = [GC * GS]

            def link(ins):
                ins.then_inc(S["t_q"], 1)
                q[0] += 1
                dve.wait_ge(S["t_q"], q[0])

            X = mybir.AxisListType.X
            def bc(v):
                return v[:].unsqueeze(2).broadcast_to([128, NT, E8])
            dn = down[:].unsqueeze(1).broadcast_to([128, NT, E8])
            dve.wait_ge(S["t_rt"], 1)
            nb_ = NT // 2
            for v in range(2):
                link(nc.vector.tensor_copy(lg[:, v * nb_:(v + 1) * nb_, :], bank[4 + v][:, 0:nb_ * E8].rearrange("p (t e) -> p t e", e=E8)))
            link(nc.vector.tensor_reduce(r1[:], lg[:], X, ALU.max))
            nc.vector.tensor_tensor(pr[:], lg[:], bc(r1), ALU.subtract).then_inc(S["t_lg"], 1)
            dve.wait_ge(S["t_ex"], 1)
            link(nc.vector.tensor_reduce(r2[:], pr[:], X, ALU.add))
            link(nc.vector.reciprocal(r2[:], r2[:]))
            link(nc.vector.tensor_tensor(pr[:], pr[:], bc(r2), ALU.mult))
            link(nc.vector.tensor_reduce(r1[:], pr[:], X, ALU.max))
            for v in range(2):
                src = pr if v == 0 else lg
                link(nc.vector.tensor_tensor(oh[:], src[:], bc(r1), ALU.is_equal))
                link(nc.vector.tensor_tensor(oh[:], oh[:], dn, ALU.mult))
                link(nc.vector.tensor_reduce(r3[:], oh[:], X, ALU.max))
                link(nc.vector.tensor_tensor(oh[:], oh[:], bc(r3), ALU.is_equal))
                if v == 0:
                    link(nc.vector.tensor_copy(cb[:], oh[:]))
                    link(nc.vector.tensor_copy(r2[:], r1[:]))
                    link(nc.vector.scalar_tensor_tensor(lg[:].rearrange("p t e -> p (t e)"), oh[:].rearrange("p t e -> p (t e)"), -2.0,
                                                        pr[:].rearrange("p t e -> p (t e)"), ALU.mult, ALU.add))
                    link(nc.vector.tensor_reduce(r1[:], lg[:], X, ALU.max))
            link(nc.vector.tensor_tensor(cb[:], cb[:], oh[:], ALU.add))
            link(nc.vector.tensor_tensor(cb[:], cb[:], pr[:], ALU.mult))
            link(nc.vector.tensor_tensor(r2[:], r2[:], r1[:], ALU.add))
            link(nc.vector.tensor_scalar(r2[:], r2[:], 1e-12, None, ALU.max))
            link(nc.vector.reciprocal(r2[:], r2[:]))
            link(nc.vector.tensor_tensor(cb[:], cb[:], bc(r2), ALU.mult))

            def experts(i, k, i0):
                for b in range(2):
                    for t in range(TILES):
                        n = i * (2 * TILES) + (b * TILES + t)
                        n0 = i0 * 2 * TILES + b * TILES + t
                        v = t % 2
                        dve.wait_ge(S["t_ps"], n + 1)
                        nc.vector.tensor_tensor(pd[v][:], bank[4 + v][:].rearrange("p (e d) -> p e d", e=E8),
                                                cb[:, bass.ds((i * TILES + t) * 2 + b, 1), :].rearrange("p t e -> p (t e)").unsqueeze(2).broadcast_to([128, E8, HALF]), ALU.mult).then_inc(S["t_pm"], 1)
                        dve.wait_ge(S["t_pm"], n + 1)
                        nc.vector.tensor_reduce(rd[v][:], pd[v][:].rearrange("p e d -> p d e"), X, ALU.add).then_inc(S["t_rd"], 1)
                        dve.wait_ge(S["t_rd"], n + 1)
                        if b == 0 and t == 0:
                            wait(dve, f"t_o{k}", (i - k) * 8, i0 - 1)
                        nc.vector.tensor_tensor(ob[k][:, t, 64 * b:64 * b + 64], rd[v][:], bank[6 + v][:, 0:HALF], ALU.add).then_inc(S["t_ob"], 1)
            run2(dve, NG, experts)

        @block.scalar
        def _(act):
            act.wait_ge(S["t_c"], NC_)
            act.wait_ge(S["t_z"], 8)

            def square(pre):
                def body(i, k, i0):
                    act.wait_ge(S[pre + "_xc"], i + 1)
                    wait(act, pre + "_var", i - 1, i0 - 1)
                    nc.scalar.activation(sq[k][:], xT[:, cols(i)], ACT.Square).then_inc(S[pre + "_sq"], 1)
                return body

            def root(pre):
                def body(i, k, i0):
                    act.wait_ge(S[pre + "_var"], i + 1)
                    wait(act, pre + "_xn", i - 1, i0 - 1)
                    nc.scalar.activation(sd[k][:], bank[4 + k][:], ACT.Sqrt, bias=eps[:, 0:1]).then_inc(S[pre + "_sd"], 1)
                return body

            def norm(pre):
                skewed(act, NG, square(pre), root(pre))

            act.wait_ge(S["t_c"], NC_)
            norm("t")
            act.wait_ge(S["t_w"], 7)

            def gates(i, k, i0, piece):
                if piece < 2:
                    act.wait_ge(S["t_h1"], i * 2 + (piece + 1))
                    wait(act, "t_gxm", i * 3, i0 * 3)
                    nc.scalar.activation(hg[piece][:], bank[piece][:, 0:GN], ACT.Gelu, bias=b1[:, 0:1]).then_inc(S["t_gel"], 1)
                else:
                    g = piece - 2
                    act.wait_ge(S["t_gxm"], i * 3 + (g + 1))
                    wait(act, "t_rn", (i - 1) * GS, (i0 - 1) * GS)
                    nc.scalar.activation(gx[k][:, :, g if g < 2 else 3, :], bank[4 + g % 2][:, 0:GN].rearrange("p (s n) -> p s n", s=GS),
                                         ACT.Identity, bias=bih[:, g:g + 1]).then_inc(S["t_gx"], 1)

            for piece in range(5):
                gates(0, 0, 0, piece)

            def gru(i, k, i0, more=True):
                for s in range(GS):
                    m = i * GS + s
                    g_ps = bank[2 + (s + k) % 2]
                    act.wait_ge(S["t_pg"], m + 1)
                    nc.scalar.activation(rzt[:], g_ps[:, 0:64].rearrange("p (g n) -> p g n", g=2), ACT.Tanh, scale=0.5).then_inc(S["t_rz"], 1)
                    act.wait_ge(S["t_rz"], m + 1)
                    wait(act, "t_nb", m, i0 * GS + s)
                    nc.scalar.activation(zb[:], rzt[:, 1], ACT.Identity, scale=-1.0, bias=one[:, 0:1]).then_inc(S["t_zb"], 1)
                    act.wait_ge(S["t_rn"], m + 1)
                    nc.scalar.activation(nt[:], nt[:], ACT.Tanh).then_inc(S["t_nt"], 1)
                    if more and s in (1, 3, 5, 7, 9):
                        gates(i + 1, 1 - k, i0 + 1, s // 2)
            run2(act, GC - 1, gru)
            gru(GC - 1, 0, GC - 1, False)

            norm("t2")
            act.wait_ge(S["t_lg"], 1)
            nc.scalar.activation(pr[:], pr[:], ACT.Exp).then_inc(S["t_ex"], 1)

            def experts(i, k, i0):
                for b in range(2):
                    for m in range(4):
                        n = i * 8 + (b * 4 + m)
                        act.wait_ge(S["t_e1"], n + 1)
                        if m == 0:
                            wait(act, "t_ps", (i * 2 + (b - 1)) * TILES, (i0 * 2 + b - 1) * TILES)
                        nc.scalar.activation(he[b][:, m, :], bank[m % 2][:], ACT.Gelu, bias=eb1[:, m:m + 1]).then_inc(S["t_eg"], 1)
            run2(act, NG, experts)

        @block.tensor
        def _(pe):
            pe.wait_ge(S["t_c"], NC_)
            pe.wait_ge(S["t_z"], 8)

            def transpose_y(i, k, i0):
                pe.wait_ge(S[f"t_y{k}"], (i - k) * 8 + (32 if i0 == NG - 1 else 16))
                wait(pe, "t_h", i - 1, i0 - 1)
                for t in range(TILES):
                    last = nc.tensor.matmul(bank[k][:, t * 128:(t + 1) * 128], yl[k][:, t, :], ident[:], start=True, stop=True)
                last.then_inc(S["t_tr"], 1)

            def mean(pre, i, k, i0):
                if pre == "t":
                    pe.wait_ge(S["t_h"], i + 1)
                wait(pe, pre + "_xc", i - 1, i0 - 1)
                nc.tensor.matmul(bank[2 + k][:], ones[:], hT[:, cols(i)], start=True, stop=True).then_inc(S[pre + "_mean"], 1)

            def var(pre, i, k, i0):
                pe.wait_ge(S[pre + "_sq"], i + 1)
                wait(pe, pre + "_sd", i - 1, i0 - 1)
                nc.tensor.matmul(bank[4 + k][:], ones[:], sq[k][:], start=True, stop=True).then_inc(S[pre + "_var"], 1)

            def mean_of(pre):
                return lambda i, k, i0: mean(pre, i, k, i0)

            def var_of(pre):
                return lambda i, k, i0: var(pre, i, k, i0)

            transpose_y(0, 0, 0)
            transpose_y(1, 1, 1)

            def ahead(i, k, i0):
                mean("t", i, k, i0)
                if i0 + 2 < NG:
                    transpose_y(i + 2, k, i0 + 2)
            ahead(0, 0, 0)

            def both(i, k, i0):
                ahead(i + 1, 1 - k, i0 + 1)
                var("t", i, k, i0)
            run2(pe, NG - 4, both)
            for i in range(NG - 4, NG - 1):
                both(i, i % 2, i)
            var("t", NG - 1, (NG - 1) % 2, NG - 1)

            pe.wait_ge(S["t_w"], 7)
            pe.wait_ge(S["t_xn"], NG)
            pe.wait_ge(S["t_sd"], NG)

            def inputs(i, k, i0, piece):
                if piece < 2:
                    wait(pe, "t_gel", i * 2, i0 * 2)
                    nc.tensor.matmul(bank[piece][:, 0:GN], w1t[:, piece, :], xT[:, cols(i, GN)], start=True, stop=True).then_inc(S["t_h1"], 1)
                else:
                    g = piece - 2
                    if g == 0:
                        pe.wait_ge(S["t_gel"], i * 2 + 2)
                    wait(pe, "t_gx", i * 3 + (0, 0, 1)[g], i0 * 3 + (0, 0, 1)[g])
                    for b in range(2):
                        last = nc.tensor.matmul(bank[4 + g % 2][64 * b:64 * b + 64, 0:GN], wih[:, 64 * g:64 * g + 64], hg[b][:], start=True, stop=True)
                    last.then_inc(S["t_gxm"], 1)

            for piece in range(5):
                inputs(0, 0, 0, piece)

            def gru(i, k, i0, more=True):
                for s in range(GS):
                    m, m0 = i * GS + s, i0 * GS + s
                    g_ps = bank[2 + (s + k) % 2]
                    before = hs[k][:, s - 1, :] if s else hs[1 - k][:, GS - 1, :]
                    if s == 0:
                        pe.wait_ge(S["t_gx"], i * 3 + 3)
                    wait(pe, "t_rh", m - 1, m0 - 1)
                    nc.tensor.matmul(g_ps[:, 0:96], ident[:], gx[k][:, s, 0:3, :], start=True, stop=False)
                    wait(pe, "t_hs", m, m0)
                    for g in range(3):
                        last = nc.tensor.matmul(g_ps[:, 32 * g:32 * g + 32], whh[:, g, :], before, start=False, stop=(g == 2))
                    last.then_inc(S["t_pg"], 1)
                    if more and s in (0, 2, 4, 6, 8):
                        inputs(i + 1, 1 - k, i0 + 1, s // 2)
            run2(pe, GC - 1, gru)
            gru(GC - 1, 0, GC - 1, False)

            pe.wait_ge(S["t_h4"], GC)

            skewed(pe, NG, mean_of("t2"), var_of("t2"))

            pe.wait_ge(S["t2_xn"], NG)
            pe.wait_ge(S["t2_sd"], NG)
            for n in range(NT // 2):
                last = nc.tensor.matmul(bank[4 + n // (NT // 4)][:, n % (NT // 4) * 2 * E8:(n % (NT // 4) + 1) * 2 * E8], xT[:, n * 128:(n + 1) * 128],
                                        rw[:].rearrange("p b e -> p (b e)"), start=True, stop=True)
            last.then_inc(S["t_rt"], 1)
            pe.wait_ge(S["t2_s"], NG)

            def up(i, b, m, i0):
                n, n0 = i * 8 + (b * 4 + m), i0 * 8 + b * 4 + m
                wait(pe, "t_eg", n - 1, n0 - 1)
                nc.tensor.matmul(bank[m % 2][:], ew1[:, b, m, :], xT[:, cols(i)], start=True, stop=True).then_inc(S["t_e1"], 1)

            def down_one(i, k, b, j, i0):
                h = slice(64 * b, 64 * b + 64)
                n, n0 = i * 8 + (b * 4 + j), i0 * 8 + b * 4 + j
                v = j % 2
                if j == 0:
                    pe.wait_ge(S["t_eg"], (i * 2 + (b + 1)) * 4)
                    pe.wait_ge(S["t_cp"], i + 1)
                wait(pe, "t_ob", n - 1, n0 - 1)
                nc.tensor.matmul(bank[6 + v][:, 0:HALF], hcp[k][h, j * 128:(j + 1) * 128], ident[h, h], start=True, stop=True)
                nc.tensor.matmul(bank[4 + v][:], one1[0:1, :], eb2[0:1, :], start=True, stop=False)
                for m in range(4):
                    last = nc.tensor.matmul(bank[4 + v][:, m * 128:(m + 1) * 128], he[b][:, m, j * 128:(j + 1) * 128], ew2[:, m, :], start=False, stop=(m == 3))
                last.then_inc(S["t_ps"], 1)

            for m in range(4):
                up(0, 0, m, 0)

            def experts(i, k, i0, more=True):
                for j in range(4):
                    up(i, 1, j, i0)
                    down_one(i, k, 0, j, i0)
                for j in range(4):
                    if more:
                        up(i + 1, 0, j, i0 + 1)
                    down_one(i, k, 1, j, i0)
            run2(pe, NG - 2, experts)
            experts(NG - 2, 0, NG - 2)
            experts(NG - 1, 1, NG - 1, False)


def program(nc, io):
    io["y2"] = nc.dram_tensor("y2", [CHUNKS[2] * T, PAIRS, 128], FP32, kind="Internal").ap()
    io["x2"] = nc.dram_tensor("x2", [CHUNKS[2], 128, COLS], FP32, kind="Internal").ap()
    build(nc, io)
    tail(nc, io)


def kernel(**inputs):
    import numpy as np
    import ml_dtypes
    import concourse.bacc as bacc
    from concourse.bass_utils import run_bass_kernel_spmd
    inp = {k: np.asarray(v) for k, v in inputs.items()}
    c0 = CHUNKS[0]
    f = np.float32

    def lay(a):
        return np.ascontiguousarray(a)

    sel = np.zeros((128, 128), ml_dtypes.bfloat16)
    for q in range(4):
        for b in range(2):
            sel[32 * q + 3 * b:32 * q + 3 * b + 3, 64 * b:64 * b + 64] = 1
    mean = np.zeros((128, 128), f)
    mean[0:64, 0:64] = mean[64:128, 64:128] = 1.0 / HALF
    arrays = {
        "xT": lay(inp["x"].reshape(2, PAIRS, c0, T, HALF).transpose(2, 0, 4, 3, 1).reshape(c0, 128, COLS)),
        "AlogT": lay(inp["L0_tok_A_log"].transpose(0, 2, 1)),
        "D": lay(inp["L0_tok_D"].T),
        "Wr": lay(inp["L0_tok_W_dbc"][:, 0, :].T),
        "WT": lay(inp["L0_tok_W_dbc"].transpose(0, 2, 1)),
        "Wdt": lay(inp["L0_tok_W_dt"][:, :, 0].T),
        "bdt": lay(inp["L0_tok_b_dt"].T),
        "sel": sel,
        "ident": np.eye(128, dtype=f),
        "W1T": lay(inp["L0_attn_W1"].T),
        "b1": lay(inp["L0_attn_b1"][:, None]),
        "WihT": lay(inp["L0_attn_W_ih"].T),
        "bih": lay(inp["L0_attn_b_ih"].reshape(3, HALF).T),
        "WhhT": lay(inp["L0_attn_W_hh"].T),
        "bhh": lay(inp["L0_attn_b_hh"].reshape(3, HALF).T),
        "ones64": mean,
        "ew1": lay(inp["L0_ffn_w1"].transpose(1, 0, 2).reshape(HALF, 4, 128)),
        "eb1": lay(inp["L0_ffn_b1"].reshape(4, 128).T),
        "ew2": lay(inp["L0_ffn_w2"].reshape(4, 2, HALF, HALF).transpose(1, 2, 0, 3)),
        "eb2": lay(inp["L0_ffn_b2"].reshape(1, 512)),
        "one1": np.ones((1, 128), f),
        "rwT": lay(inp["L0_ffn_router_w"].T),
        "down": np.tile(np.arange(8, 0, -1, dtype=f), (128, 1)),
    }
    nc = bacc.Bacc("TRN2", target_bir_lowering=False, num_devices=1)
    io = {k: nc.dram_tensor(k + "_in", a.shape, mybir.dt.from_np(a.dtype), kind="ExternalInput").ap() for k, a in arrays.items()}
    io["out"] = nc.dram_tensor("out", (TOK, 128), FP32, kind="ExternalOutput").ap()
    program(nc, io)
    r = run_bass_kernel_spmd(nc, [{k + "_in": a for k, a in arrays.items()}], core_ids=[0])
    out = r.results[0]["out"][:NTOK].reshape(SEQ[2], PAIRS, 2, HALF)
    return lay(out.transpose(2, 1, 0, 3).reshape(64, SEQ[2], HALF))
```

```python
import concourse.bass as bass
from concourse import mybir
from contextlib import ExitStack

FP32 = mybir.dt.float32
BF16 = mybir.dt.bfloat16
ALU = mybir.AluOpType
ACT = mybir.ActivationFunctionType

HALF = 64
PAIRS = 32
T = 5
COLS = T * PAIRS
SEQ = [750, 375, 187]
CHUNKS = [-(-s // T) for s in SEQ]
FIRST = [0, CHUNKS[0], CHUNKS[0] + CHUNKS[1]]
TOTAL = sum(CHUNKS)
SLOTS = 2 * T
YROWS = 80
YT = 2 * COLS // YROWS
STEPS = HALF // 2
SPARE = slice(2 * COLS, 3 * COLS)
Z_STEP, B_STEP, C_STEP, P0_STEP, P1_STEP, TR_STEP = 2, 3, 1, 13, 17, 30
DX_STEPS = (0, 4, 7, 10, 13, 17, 20, 23, 26, 29)
Y_STEPS = range(4, 31)


def layer_of(g):
    return 2 if g >= FIRST[2] else 1 if g >= FIRST[1] else 0


def ssm(nc, io):
    ctx = ExitStack()
    with ctx:
        def sb(name, shape, dt=FP32):
            return ctx.enter_context(nc.sbuf_tensor(name, shape, dt))

        def ps(name, shape):
            return ctx.enter_context(nc.psum_tensor(name, shape, FP32))

        def sem(name):
            return ctx.enter_context(nc.semaphore(name))

        xT, AlogT, Dp, WT, Wr, Wdt, bdt, sel_d, id_d = (io[k] for k in ("xT", "AlogT", "D", "WT", "Wr", "Wdt", "bdt", "sel", "ident"))
        y_dram = [nc.dram_tensor(f"y{i}", [CHUNKS[i] * T, PAIRS, 128], FP32, kind="Internal").ap() for i in range(2)]
        y_dram.append(io["y2"])
        x_dram = [xT, nc.dram_tensor("x1", [CHUNKS[1], 128, COLS], FP32, kind="Internal").ap(), io["x2"]]

        hb = [sb(f"h{k}", [128, HALF, T, PAIRS]) for k in range(3)]
        row = [sb(f"row{k}", [128, 16, 2, COLS], BF16) for k in range(3)]
        cz = [sb(f"cz{k}", [128, PAIRS, 32]) for k in range(3)]
        xin = [sb(f"xin{k}", [128, COLS]) for k in range(3)]
        bt = [sb(f"bt{k}", [128, COLS]) for k in range(3)]
        zt = sb("zt", [128, COLS])
        rz = sb("rz", [128, COLS])
        dd = sb("dd", [128, 2, COLS])
        d3 = sb("d3", [128, 3, 2, COLS], BF16)
        ysb = sb("ysb", [128, 8, T * HALF])
        yld = sb("yld", [YROWS, YT, 128])
        xprev = sb("xprev", [128, 2, COLS])
        wbd = sb("wbd", [128, 3, 3, 128])
        wr = sb("wr", [128, 3])
        at = sb("at", [128, 3, HALF])
        dsk = sb("dsk", [128, 3])
        wdt = sb("wdt", [128, 3])
        bd = sb("bd", [128, 3])
        sel = sb("sel", [128, 128], BF16)
        ident = sb("ident", [128, 128])
        psX = ps("psX", [128, 2, 32, PAIRS])
        psD = [ps(f"psD{k}", [128, 512]) for k in range(2)]
        psC = [ps(f"psC{k}", [128, 512]) for k in range(2)]

        S = {n: sem(n) for n in (
            "s_const s_wz s_wd s_wrep s_ea s_at s_xt0 s_xt1 s_xt2 s_yl s_xp s_tr s_xo s_xs s_xin s_x1s s_rb s_za s_rz s_zl s_bt s_dl s_dd s_p0 "
            "s_r1 s_bb s_p1 s_p2 s_row0 s_row1 s_row2 s_cp s_cz s_db s_exp s_dxb s_m s_u s_h s_c s_ev s_y0 s_y1 s_psz").split()}
        s_row = [S["s_row0"], S["s_row1"], S["s_row2"]]
        s_xt = [S["s_xt0"], S["s_xt1"], S["s_xt2"]]
        s_y = [S["s_y0"], S["s_y1"]]
        block = ctx.enter_context(nc.Block())
        N_CONST = 10

        turn = [0]
        def plan():
            out = [("one", p) for p in (-3, -2, -1, 0, 1)]
            for l in range(3):
                a, b = FIRST[l] + 2, FIRST[l] + CHUNKS[l] - 4
                if l == 2:
                    b -= 1
                n = (b - a + 1) // 3
                out.append(("loop", a, n))
                nxt = FIRST[l + 1] + 2 if l < 2 else TOTAL + 2
                out += [("one", p) for p in range(a + 3 * n, nxt)]
            return out

        def run(eng, period):
            def layers(p):
                return [layer_of(g) if 0 <= g < TOTAL else None for g in range(p - 1, p + 4)]
            for item in plan():
                if item[0] == "one":
                    p = item[1]
                    turn[0] = 0
                    period(p, p % 3, layers(p), p)
                else:
                    _, a, n = item
                    with eng.Fori(0, n) as i:
                        turn[0] = i
                        for j in range(3):
                            period(i * 3 + (a + j), (a + j) % 3, layers(a + j), a + j)

        def wait(eng, s, value, least):
            if least > 0:
                eng.wait_ge(s, value)

        def snap(eng, v):
            return v if isinstance(v, int) else eng.snap(v)

        def thirds(c, c0):
            return turn[0] + (c0 // 3 + 1)

        def y_step(i):
            return Y_STEPS[i * len(Y_STEPS) // PAIRS]

        @block.sync
        def _(sp):
            for b in range(2):
                h = slice(b * 64, b * 64 + 64)
                sp.dma_start(at[h, :, :], AlogT.rearrange("l n e -> n l e")).then_inc(S["s_const"], 16)
                sp.dma_start(wr[h, :], Wr).then_inc(S["s_const"], 16)
                sp.dma_start(dsk[h, :], Dp).then_inc(S["s_const"], 16)
                sp.dma_start(wdt[h, :], Wdt).then_inc(S["s_const"], 16)
                sp.dma_start(bd[h, :], bdt).then_inc(S["s_const"], 16)
            sp.dma_start(sel[:], sel_d).then_inc(S["s_const"], 16)
            sp.dma_start(ident[:], id_d).then_inc(S["s_const"], 16)
            sp.wait_ge(S["s_wz"], 1)
            for b in range(2):
                h = slice(b * 64, b * 64 + 64)
                for l in range(3):
                    sp.dma_start(wbd[h, l, 1:3, h], WT[l, :, 1:129].rearrange("k (v n) -> k v n", v=2)).then_inc(S["s_wd"], 16)

            def load_x(c, c0, k):
                at_c, used = snap(sp, c), snap(sp, c - 2)
                wait(sp, S["s_cp"], used, c0 - 2)
                wait(sp, S["s_dd"], used, c0 - 2)
                sp.dma_start(xin[k][:], xT[bass.ds(at_c, 1), :, :].rearrange("c p n -> (c p) n")).then_inc(s_xt[k], 16)

            def load_y(c, c0, l):
                n, n0 = c - FIRST[l], c0 - FIRST[l]
                chunks = min(2, CHUNKS[l - 1] - 2 * n0)
                at_row, at_x = snap(sp, n * (2 * COLS)), snap(sp, n * 2)
                stored = snap(sp, (n * 2 + (FIRST[l - 1] + chunks)) * 80)
                x_stored = snap(sp, (n * 2 + chunks) * 16)
                used = snap(sp, c - FIRST[1])
                wait(sp, S["s_xs"], used, c0 - FIRST[1])
                sp.wait_ge(s_y[0], stored)
                sp.wait_ge(s_y[1], stored)
                if l == 2:
                    sp.wait_ge(S["s_x1s"], x_stored)
                rows = y_dram[l - 1].rearrange("t p f -> (t p) f")
                sp.dma_start(yld[:, 0:chunks * YT // 2, :],
                             rows[bass.ds(at_row, chunks * COLS), :].rearrange("(i r) f -> r i f", r=YROWS)).then_inc(S["s_yl"], 16)
                sp.dma_start(xprev[:, 0:chunks, :],
                             x_dram[l - 1][bass.ds(at_x, chunks), :, :].rearrange("c p n -> p c n")).then_inc(S["s_xp"], 16)

            def store_x(c, c0, l):
                at_c, there = snap(sp, c - FIRST[l]), snap(sp, c - (FIRST[1] - 1))
                sp.wait_ge(S["s_xin"], there)
                sp.dma_start(x_dram[l][bass.ds(at_c, 1), :, :].rearrange("c p n -> (c p) n"), xin[c0 % 3][:]).then_inc(S["s_x1s"], 16)

            def rows_out(c, c0):
                k = c0 % 3
                sp.wait_ge(S["s_p2"], c + 1)
                for b in range(2):
                    for s in range(3):
                        sp.dma_start(row[k][3 * b + s:128:32, :, :, :],
                                     d3[b * 64:b * 64 + 64, s, :, :]).then_inc(s_row[k], 16)

            def store_y(c, c0, half, l):
                at_t, there = [snap(sp, (c - FIRST[l]) * T + t) for t in range(T)], snap(sp, c * 8 + (4 * half + 4))
                sp.wait_ge(S["s_ev"], there)
                for t in range(T):
                    dst = y_dram[l][bass.ds(at_t[t], 1), 16 * half:16 * half + 16, :]
                    sp.dma_start(dst.rearrange("t (g j) (b e) -> (j t b) g e", j=4, b=2),
                                 ysb[t:128:16, 4 * half:4 * half + 4, t * HALF:(t + 1) * HALF]).then_inc(s_y[half], 16)

            def period(p, k, ls, p0):
                if 2 <= p0:
                    store_y(p - 2, p0 - 2, 1, layer_of(p0 - 2))
                c, c0 = p + 2, p0 + 2
                l = ls[3]
                if ls[4] == 0:
                    load_x(p + 3, p0 + 3, (p0 + 3) % 3)
                if ls[4]:
                    load_y(p + 3, p0 + 3, ls[4])
                if l is not None and l > 0:
                    store_x(c, c0, l)
                if l is not None:
                    rows_out(c, c0)
                if ls[0] is not None:
                    store_y(p - 1, p0 - 1, 0, ls[0])

            run(sp, period)
            for h in range(2):
                sp.wait_ge(s_y[h], 80 * TOTAL)
            sp.wait_ge(S["s_x1s"], 16 * (CHUNKS[1] + CHUNKS[2]))

        @block.gpsimd
        def _(pool):
            nc.gpsimd.memset(wbd[:], 0.0).then_inc(S["s_wz"], 1)
            for k in range(3):
                nc.gpsimd.memset(cz[k][:], 0.0).then_inc(S["s_psz"], 1)

            def period(p, k, ls, p0):
                l = ls[1]
                if l is None:
                    return
                for s in range(SLOTS):
                    t, es = s // 2, slice(32 * (s % 2), 32 * (s % 2) + 32)
                    now = hb[k][:, es, t, :]
                    if t == 0:
                        pool.wait_ge(S["s_exp"], p * 64 + 32 * (s + 1))
                        before = hb[(k + 2) % 3][:, es, T - 1, :]
                    else:
                        before = hb[k][:, es, t - 1, :]
                    if t == 0 and p0 in FIRST:
                        nc.gpsimd.memset(now, 0.0).then_inc(S["s_u"], 1)
                    else:
                        wait(pool, S["s_h"], p * SLOTS + (s - 1), p0 * SLOTS + s - 1)
                        nc.gpsimd.tensor_tensor(now, now, before, ALU.mult).then_inc(S["s_u"], 1)

            run(pool, period)

        @block.vector
        def _(dve):
            dve.wait_ge(S["s_const"], 16 * 12)
            dve.wait_ge(S["s_wz"], 1)
            for b in range(2):
                h = slice(b * 64, b * 64 + 64)
                for l in range(3):
                    nc.vector.tensor_copy(wbd[h, l, 0, h], wr[h, l:l + 1].broadcast_to([64, 64])).then_inc(S["s_wrep"], 1)
            dve.wait_ge(S["s_ea"], 1)
            nc.vector.tensor_scalar(at[:], at[:], -1.0, None, ALU.mult).then_inc(S["s_at"], 1)

            def period(p, k, ls, p0):
                c, c0, l2 = p + 2, p0 + 2, ls[3]
                kx = c0 % 3
                for s in range(SLOTS):
                    t, es = s // 2, slice(32 * (s % 2), 32 * (s % 2) + 32)
                    if ls[1] is not None:
                        n = p * SLOTS + (s + 1)
                        dve.wait_ge(S["s_dxb"], n)
                        if s == 0:
                            dve.wait_ge(S["s_bt"], p + 1)
                        b_t = bt[k][:, t * PAIRS:(t + 1) * PAIRS].unsqueeze(1).broadcast_to([128, 32, PAIRS])
                        nc.vector.tensor_tensor(psX[:, s % 2], psX[:, s % 2], b_t, ALU.mult).then_inc(S["s_m"], 1)
                        now = hb[k][:, es, t, :]
                        dve.wait_ge(S["s_m"], n)
                        dve.wait_ge(S["s_u"], n)
                        nc.vector.tensor_tensor(now, now, psX[:, s % 2], ALU.add).then_inc(S["s_h"], 1)
                    if s == 9 and ls[4]:
                        l4, n4, c4 = ls[4], p + (3 - FIRST[1]), p0 + 3 - FIRST[1]
                        dve.wait_ge(S["s_tr"], n4 + 1)
                        dve.wait_ge(S["s_xp"], (n4 + 1) * 16)
                        nc.vector.scalar_tensor_tensor(xprev[:].rearrange("p v n -> p (v n)"), xprev[:].rearrange("p v n -> p (v n)"), dsk[:, l4 - 1:l4],
                                                       psC[0][:, 0:2 * COLS], ALU.mult, ALU.add).then_inc(S["s_xo"], 1)
                        dve.wait_ge(S["s_xo"], n4 + 1)
                        dve.wait_ge(S["s_cp"], p + 1)
                        wait(dve, S["s_x1s"], (n4 - 2) * 16, (c4 - 2) * 16)
                        pairs = xprev[:].rearrange("p v (t n) -> p (v t) n", t=T)
                        nc.vector.tensor_tensor(xin[k][:].rearrange("p (t n) -> p t n", t=T), pairs[:, 0:2 * T:2, :], pairs[:, 1:2 * T:2, :],
                                                ALU.add).then_inc(S["s_xs"], 1)
                    if l2 is None:
                        continue
                    if s == 3:
                        dve.wait_ge(S["s_zl"], c + 1)
                        dve.wait_ge(S["s_rz"], c + 1)
                        wait(dve, S["s_p2"], c, c0)
                        nc.vector.tensor_tensor(dd[:, 0, :], zt[:], rz[:], ALU.add).then_inc(S["s_dl"], 1)
                        dve.wait_ge(S["s_dl"], c + 1)
                        nc.vector.tensor_tensor(dd[:, 1, :], dd[:, 0, :], xin[kx][:], ALU.mult).then_inc(S["s_dd"], 1)
                    if s == 4:
                        dve.wait_ge(S["s_p0"], c + 1)
                        nc.vector.tensor_tensor(dd[:], dd[:], d3[:, 0], ALU.subtract).then_inc(S["s_r1"], 1)
                    if s == 5:
                        dve.wait_ge(S["s_p1"], c + 1)
                        nc.vector.tensor_tensor(d3[:, 2], dd[:], d3[:, 1], ALU.subtract).then_inc(S["s_p2"], 1)

            run(dve, period)

        @block.scalar
        def _(act):
            act.preload_act_table_set("natural_log_exp_and_others")
            act.wait_ge(S["s_const"], 16 * 12)
            nc.scalar.activation(at[:], at[:], ACT.Exp).then_inc(S["s_ea"], 1)
            act.wait_ge(S["s_at"], 1)

            def period(p, k, ls, p0):
                c, c0, l2 = p + 2, p0 + 2, ls[3]
                kx = c0 % 3
                ke = (k + 1) % 3
                for i in range(STEPS):
                    if i == 0 and l2:
                        act.wait_ge(S["s_xs"], c - (FIRST[1] - 1))
                        nc.scalar.activation(xin[kx][:], xin[kx][:], ACT.Copy, scale=0.5).then_inc(S["s_xin"], 1)
                    if i == 0 and ls[2] is not None:
                        wait(act, S["s_c"], (p - 1) * 8, (p0 - 1) * 8)
                        wait(act, S["s_u"], (p - 1) * SLOTS + 2, (p0 - 1) * SLOTS + 2)
                    if i == Z_STEP and l2 is not None:
                        wait(act, S["s_dl"], c, c0)
                        act.wait_ge(S["s_rb"], c + 1)
                        z = psD[i % 2][:, SPARE]
                        nc.scalar.activation(zt[:], z, ACT.Abs, bias=bd[:, l2:l2 + 1], scale=wdt[:, l2:l2 + 1]).then_inc(S["s_za"], 1)
                        nc.scalar.activation(rz[:], z, ACT.Relu, bias=bd[:, l2:l2 + 1], scale=wdt[:, l2:l2 + 1]).then_inc(S["s_rz"], 1)
                    if i == B_STEP and l2 is not None:
                        act.wait_ge(S["s_za"], c * 2 + 1)
                        nc.scalar.activation(zt[:], zt[:], ACT.Exp, scale=-1.0).then_inc(S["s_za"], 1)
                        act.wait_ge(S["s_bb"], c + 1)
                        wait(act, S["s_m"], (c - 2) * SLOTS, (c0 - 2) * SLOTS)
                        nc.scalar.activation(bt[kx][:], psD[i % 2][:, SPARE], ACT.Copy).then_inc(S["s_bt"], 1)
                    if i == B_STEP + 1 and l2 is not None:
                        act.wait_ge(S["s_za"], c * 2 + 2)
                        nc.scalar.activation(zt[:], zt[:], ACT.Ln, bias=1.0).then_inc(S["s_zl"], 1)
                    if i == C_STEP and ls[1] is not None:
                        act.wait_ge(S["s_cp"], p + 1)
                        for b in range(2):
                            h = slice(b * 64, b * 64 + 64)
                            nc.scalar.activation(cz[k][h, :, 16 * b:16 * b + T], psD[i % 2][h, SPARE].rearrange("p (t n) -> p n t", t=T),
                                                 ACT.Copy).then_inc(S["s_cz"], 1)
                    if i == P0_STEP and l2 is not None:
                        act.wait_ge(S["s_dd"], c + 1)
                        if c0 > 0:
                            act.wait_ge(s_row[(c0 - 1) % 3], thirds(c - 1, c0 - 1) * 96)
                        nc.scalar.activation(d3[:, 0], dd[:], ACT.Copy).then_inc(S["s_p0"], 1)
                    if i == P1_STEP and l2 is not None:
                        act.wait_ge(S["s_r1"], c + 1)
                        nc.scalar.activation(d3[:, 1], dd[:], ACT.Copy).then_inc(S["s_p1"], 1)
                    if ls[2] is not None:
                        act.wait_ge(S["s_db"], (p + 1) * STEPS + (i + 1))
                        for e in (2 * i, 2 * i + 1):
                            nc.scalar.activation(hb[ke][:, e], psD[i % 2][:, (e % 2) * COLS:(e % 2 + 1) * COLS].rearrange("p (t n) -> p t n", t=T),
                                                 ACT.Exp, scale=at[:, ls[2], e:e + 1]).then_inc(S["s_exp"], 1)
                    for g in range(8):
                        if ls[0] is not None and i == y_step(4 * g + 3) + 1:
                            evac(p - 1, p0 - 1, g)

            def evac(c, c0, g):
                act.wait_ge(S["s_c"], c * 8 + (g + 1))
                if g % 4 == 0:
                    wait(act, s_y[g // 4], c * 80, c0)
                nc.scalar.activation(ysb[:, g, :], psC[g % 2][:, 0:T * HALF], ACT.Copy).then_inc(S["s_ev"], 1)

            run(act, period)

        @block.tensor
        def _(pe):
            pe.wait_ge(S["s_const"], 16 * 12)
            pe.wait_ge(S["s_wd"], 16 * 6)
            pe.wait_ge(S["s_wrep"], 6)
            pe.wait_ge(S["s_psz"], 3)

            def dx_broadcast(c, c0, k, s):
                t = s // 2
                wait(pe, S["s_h"], c * SLOTS + (s - 1), c0 * SLOTS + s - 1)
                for q in (0, 1):
                    e4 = 2 * (s % 2) + q
                    r = slice(32 * e4, 32 * e4 + 6)
                    last = nc.tensor.matmul(psX[:, s % 2, 16 * q:16 * q + 16, :], sel[r, :], row[k][r, :, 1, t * PAIRS:(t + 1) * PAIRS],
                                            start=True, stop=True)
                last.then_inc(S["s_dxb"], 1)

            def period(p, k, ls, p0):
                c, c0, l2 = p + 2, p0 + 2, ls[3]
                kx = c0 % 3
                ke = (k + 1) % 3
                if p0 == -1:
                    pe.wait_ge(S["s_rz"], 1)
                    pe.wait_ge(S["s_za"], 1)
                    pe.wait_ge(S["s_bt"], 1)
                for i in range(STEPS):
                    for s in range(SLOTS):
                        if i == DX_STEPS[s]:
                            if s < SLOTS - 1 and ls[1] is not None:
                                dx_broadcast(p, p0, k, s + 1)
                            if s == SLOTS - 1 and ls[2] is not None:
                                dx_broadcast(p + 1, p0 + 1, ke, 0)
                    if ls[2] is not None:
                        if i == Z_STEP + 2 and l2 is not None:
                            pe.wait_ge(S["s_rz"], c + 1)
                            pe.wait_ge(S["s_za"], c * 2 + 1)
                        if i == B_STEP + 2 and l2 is not None:
                            pe.wait_ge(S["s_bt"], c + 1)
                        if i == C_STEP + 2 and ls[1] is not None:
                            pe.wait_ge(S["s_cz"], p * 2 + 2)
                        delta_broadcast(p + 1, p0 + 1, ke, i)
                    if i == Z_STEP and l2 is not None:
                        if l2 == 0:
                            pe.wait_ge(s_xt[kx], thirds(c, c0) * 16)
                        else:
                            pe.wait_ge(S["s_xin"], c - (FIRST[1] - 1))
                        nc.tensor.matmul(psD[i % 2][:, SPARE], wbd[:, l2, 0, :], xin[kx][:], start=True, stop=True).then_inc(S["s_rb"], 1)
                    if i == B_STEP and l2 is not None:
                        nc.tensor.matmul(psD[i % 2][:, SPARE], wbd[:, l2, 1, :], xin[kx][:], start=True, stop=True).then_inc(S["s_bb"], 1)
                    if i == C_STEP and ls[1] is not None:
                        if ls[2] is None:
                            pe.wait_ge(S["s_exp"], (p + 1) * HALF)
                        nc.tensor.matmul(psD[i % 2][:, SPARE], wbd[:, ls[1], 2, :], xin[k][:], start=True, stop=True).then_inc(S["s_cp"], 1)
                    if i == TR_STEP and ls[4]:
                        n4 = p + (3 - FIRST[1])
                        pe.wait_ge(S["s_yl"], (n4 + 1) * 16)
                        pe.wait_ge(S["s_ev"], (p - 1) * 8 + 7)
                        for j in range(YT):
                            last = nc.tensor.transpose(psC[0][:, j * YROWS:(j + 1) * YROWS], yld[:, j, :], ident[0:YROWS, 0:YROWS])
                        last.then_inc(S["s_tr"], 1)
                    if ls[0] is not None:
                        for j in range(PAIRS):
                            if y_step(j) == i:
                                y_matmul(p - 1, p0 - 1, (k + 2) % 3, j)

            def delta_broadcast(c, c0, k, ep):
                if ep == 0:
                    pe.wait_ge(s_row[k], thirds(c, c0) * 96)
                if c0 > 0 or ep >= 2:
                    pe.wait_ge(S["s_exp"], c * 64 + 2 * (ep - 1))
                r = slice(32 * (ep // 8), 32 * (ep // 8) + 6)
                nc.tensor.matmul(psD[ep % 2][:, 0:2 * COLS], sel[r, :], row[k][r, 2 * (ep % 8):2 * (ep % 8) + 2, 0, :],
                                 start=True, stop=True).then_inc(S["s_db"], 1)

            def y_matmul(c, c0, k, i):
                g, j = i // 4, i % 4
                if i == 0:
                    pe.wait_ge(S["s_h"], (c + 1) * SLOTS)
                    pe.wait_ge(S["s_cz"], (c + 1) * 2)
                if i == 0 and FIRST[1] - 3 <= c0 < TOTAL - 3:
                    pe.wait_ge(S["s_xo"], c + (4 - FIRST[1]))
                if j == 0 and (c0 > 0 or g >= 2):
                    pe.wait_ge(S["s_ev"], c * 8 + (g - 1))
                last = nc.tensor.matmul(psC[g % 2][32 * j:32 * j + 32, 0:T * HALF], cz[k][:, i, :], hb[k][:, :, :, i].rearrange("p e t -> p t e"),
                                        start=True, stop=True)
                if j == 3:
                    last.then_inc(S["s_c"], 1)

            run(pe, period)


GS = 11
GC = SEQ[2] // GS
GN = GS * PAIRS
NTOK = SEQ[2] * PAIRS
GROUP = 512
NG = -(-NTOK // GROUP)
TOK = NG * GROUP
TILES = GROUP // 128
PIECE_AT = (0, 2, 4, 6, 8, 9)
PIECES = len(PIECE_AT)
SEQS = 2 * PAIRS
E8 = 8
EPS = 1e-5


def tail(nc, io):
    ctx = ExitStack()
    with ctx:
        def sb(name, shape, dt=FP32):
            return ctx.enter_context(nc.sbuf_tensor(name, shape, dt))

        def ps(name, shape):
            return ctx.enter_context(nc.psum_tensor(name, shape, FP32))

        def sem(name):
            return ctx.enter_context(nc.semaphore(name))

        hT = sb("hT", [128, TOK])
        xT = sb("xnT", [128, TOK])
        yl = [sb(f"yl{k}", [128, TILES, 128]) for k in range(2)]
        sq = [sb(f"sq{k}", [128, GROUP]) for k in range(2)]
        sd = [sb(f"sd{k}", [128, GROUP]) for k in range(2)]
        hg = [sb(f"hg{b}", [128, GN]) for b in range(2)]
        grz = [sb(f"grz{k}", [128, GS, SEQS]) for k in range(2)]
        gn = [sb(f"gn{k}", [HALF, GS, SEQS]) for k in range(2)]
        cn = sb("cn", [HALF, SEQS])
        hs = [sb(f"hs{k}", [HALF, GS, SEQS]) for k in range(2)]
        hx = sb("hx", [128, GS, PAIRS])
        eps = sb("eps", [128, 1])
        hcp = [sb(f"hcp{k}", [128, GROUP]) for k in range(2)]
        rt = sb("rt", [HALF, SEQS])
        zt = sb("gzt", [HALF, SEQS])
        nt = sb("nt", [HALF, SEQS])
        nb = sb("nb", [HALF, SEQS])
        za = sb("gza", [HALF, SEQS])
        w1t = sb("w1t", [128, 2, 128])
        b1 = sb("gb1", [128, 1])
        wih = sb("wih", [128, 192])
        whh = sb("whh", [HALF, 192])
        brz = sb("brz", [128, 2])
        bn = sb("bn", [HALF, 2])
        ident = sb("tident", [128, 128])
        ones = sb("ones64", [128, 128])
        dsk = sb("tdsk", [128, 3])
        ew1 = sb("ew1", [128, 2, 4, 128])
        eb1 = sb("eb1", [128, 4])
        ew2 = sb("ew2", [128, 4, 128])
        eb2 = sb("eb2", [1, 512])
        eb2p = sb("eb2p", [1, 3, 512], BF16)
        eb2r = sb("eb2r", [3, 512], BF16)
        one3 = sb("one3", [3, 128], BF16)
        rw = sb("rw", [128, 2, E8])
        down = sb("down", [128, E8])
        NT = NG * TILES * 2
        lg = sb("lg", [128, NT, E8])
        pr = sb("pr", [128, NT, E8])
        oh = sb("oh", [128, NT, E8])
        cb = sb("cb", [128, NT, E8])
        r1 = sb("r1v", [128, NT])
        r2 = sb("r2v", [128, NT])
        r3 = sb("r3v", [128, NT])
        he = [sb(f"he{k}", [128, 4, GROUP]) for k in range(2)]
        pd = [sb(f"pd{k}", [128, E8, HALF]) for k in range(2)]
        rd = [sb(f"rd{k}", [128, HALF]) for k in range(2)]
        ob = [sb(f"ob{k}", [128, TILES, 128]) for k in range(2)]
        bank = [ps(f"bank{k}", [128, 512]) for k in range(8)]

        names = ("t_c t_z t_w t_y0 t_y1 t_tr t_h t_mean t_xc t_sq t_var t_sd t_rs t_xn t_h1 t_gel t_gxm t_gx t_pg t_pn t_rz t_gz t_rh t_rn t_nt t_hc t_b3 t_br "
                 "t_nb t_hs t_h4 t2_mean t2_xc t2_sq t2_var t2_sd t2_rs t2_xn t_rt t_cp t_lg t_q t_ex t_e1 t_eg t_ps t_pm t_rd t_ob t_o0 t_o1").split()
        S = {n: sem(n) for n in names}
        yrows = io["y2"].rearrange("t p f -> (t p) f")
        block = ctx.enter_context(nc.Block())
        NLOAD = 26

        def run2(eng, n, body, start=0):
            if start == 0:
                body(0, 0, 0)
                body(1, 1, 1)
                start = 2
            with eng.Fori(start // 2, n // 2) as j:
                for u in range(2):
                    body(j * 2 + u, u, start + u)
            if n % 2:
                body(n - 1, 0, n - 1)

        def skewed(eng, n, first, second):
            first(0, 0, 0)

            def both(i, k, i0):
                first(i + 1, 1 - k, i0 + 1)
                second(i, k, i0)
            run2(eng, n - 1, both)
            second(n - 1, (n - 1) % 2, n - 1)

        def wait(eng, s, value, least):
            if least > 0:
                eng.wait_ge(S[s], value)

        def cols(i, n=GROUP, off=0):
            return bass.ds(i * n + off, n)

        @block.sync
        def _(sp):
            n = 0
            def load(dst, src):
                nonlocal n
                n += 1
                sp.dma_start(dst, src).then_inc(S["t_c"], 16)
            for b in range(2):
                h = slice(64 * b, 64 * b + 64)
                load(brz[h, 0:1], io["bih"][b])
                load(brz[h, 1:2], io["bhh"][b])
                load(dsk[h, :], io["D"])
            load(bn[:, 0:1], io["bih"][2])
            load(bn[:, 1:2], io["bhh"][2])
            load(whh[:], io["WhhT"])
            load(b1[:], io["b1"])
            load(wih[:], io["WihT"])
            load(ident[:], io["ident"])
            load(ones[:], io["ones64"])
            load(eb1[:], io["eb1"])
            load(eb2[:], io["eb2"])
            load(one3[:], io["one3"])
            load(down[:], io["down"])
            load(hT[:, 0:CHUNKS[2] * COLS].rearrange("p (c n) -> p c n", n=COLS), io["x2"].rearrange("c p n -> p c n"))
            sp.wait_ge(S["t_z"], 6)
            for b in range(2):
                h = slice(64 * b, 64 * b + 64)
                load(ew2[h, :, h], io["ew2"][b])
                load(w1t[h, b, :], io["W1T"])
                load(rw[h, b, :], io["rwT"])
                load(ew1[h, b, :, :], io["ew1"])
            assert n == NLOAD, n
            sp.wait_ge(S["t_b3"], 5)
            sp.dma_start(eb2r[:], eb2p[:]).then_inc(S["t_br"], 16)
            def load_y(i, k, i0, rows=GROUP):
                at, used = (i * GROUP, i - 1) if isinstance(i, int) else (sp.snap(i * GROUP), sp.snap(i - 1))
                wait(sp, "t_tr", used, i0 - 1)
                full = rows // 128
                sp.dma_start(yl[k][:, 0:full, :], yrows[bass.ds(at, full * 128), :].rearrange("(k r) f -> r k f", r=128)).then_inc(S[f"t_y{k}"], 16)
                if rows % 128:
                    sp.dma_start(yl[k][0:rows % 128, full, :], yrows[i * GROUP + full * 128:i * GROUP + rows, :]).then_inc(S[f"t_y{k}"], 16)
            load_y(0, 0, 0)
            load_y(1, 1, 1)
            run2(sp, NG - 2, load_y, 2)
            load_y(NG - 2, 0, NG - 2)
            load_y(NG - 1, 1, NG - 1, CHUNKS[2] * COLS - (NG - 1) * GROUP)
            def out(i, k, i0):
                at = i * GROUP if isinstance(i, int) else sp.snap(i * GROUP)
                done = (i + 1) * (2 * TILES) if isinstance(i, int) else sp.snap((i + 1) * (2 * TILES))
                sp.wait_ge(S["t_ob"], done)
                sp.dma_start(io["out"][bass.ds(at, GROUP), :].rearrange("(k r) f -> r k f", r=128), ob[k][:]).then_inc(S[f"t_o{k}"], 16)
            run2(sp, NG, out)
            sp.wait_ge(S["t_o0"], 16 * (NG // 2))
            sp.wait_ge(S["t_o1"], 16 * (NG // 2))

        NC_ = NLOAD * 16

        @block.gpsimd
        def _(pool):
            nc.gpsimd.memset(ew2[:], 0.0).then_inc(S["t_z"], 1)
            nc.gpsimd.memset(rw[:], 0.0).then_inc(S["t_z"], 1)
            nc.gpsimd.memset(w1t[:], 0.0).then_inc(S["t_z"], 1)
            nc.gpsimd.memset(ew1[:], 0.0).then_inc(S["t_z"], 1)
            nc.gpsimd.memset(hT[:, CHUNKS[2] * COLS:TOK], 0.0).then_inc(S["t_z"], 1)
            nc.gpsimd.memset(eps[:], EPS).then_inc(S["t_z"], 1)
            def add_state(i, k, i0):
                pool.wait_ge(S["t_hc"], i * 2 + 2)
                nc.gpsimd.tensor_tensor(hT[:, cols(i, GN)], hx[:].rearrange("p s n -> p (s n)"), hT[:, cols(i, GN)], ALU.add).then_inc(S["t_h4"], 1)
            run2(pool, GC, add_state)

            def copy(i, k, i0):
                pool.wait_ge(S["t2_xn"], i + 1)
                wait(pool, "t_ps", (i - 1) * 8, i0 - 1)
                nc.gpsimd.tensor_tensor(hcp[k][:], hT[:, cols(i)], xT[:, cols(i)], ALU.add).then_inc(S["t_cp"], 1)
            run2(pool, NG, copy)

        @block.vector
        def _(dve):
            dve.wait_ge(S["t_c"], NC_)
            dve.wait_ge(S["t_z"], 6)
            nc.vector.tensor_scalar(whh[:, 0:128], whh[:, 0:128], 0.5, None, ALU.mult).then_inc(S["t_w"], 1)
            nc.vector.tensor_scalar(whh[:, 128:192], whh[:, 128:192], 0.25, None, ALU.mult).then_inc(S["t_w"], 1)
            nc.vector.tensor_tensor(brz[:, 0:1], brz[:, 0:1], brz[:, 1:2], ALU.add).then_inc(S["t_w"], 1)
            nc.vector.tensor_scalar(bn[:, 1:2], bn[:, 1:2], 0.5, None, ALU.mult).then_inc(S["t_w"], 1)
            for v in range(3):
                nc.vector.tensor_copy(eb2p[:, v, :], eb2[:]).then_inc(S["t_b3"], 1)
                if v < 2:
                    dve.wait_ge(S["t_b3"], 2 * v + 1)
                    nc.vector.tensor_tensor(eb2[:], eb2[:], eb2p[:, v, :], ALU.subtract).then_inc(S["t_b3"], 1)
                    dve.wait_ge(S["t_b3"], 2 * v + 2)
            dve.wait_ge(S["t_w"], 4)
            nc.vector.tensor_copy(cn[:], bn[:, 1:2].broadcast_to([HALF, SEQS])).then_inc(S["t_w"], 1)
            nc.vector.memset(hs[1][:, GS - 1, :], 0.0).then_inc(S["t_w"], 1)

            def skip(i, k, i0):
                dve.wait_ge(S["t_tr"], i + 1)
                nc.vector.scalar_tensor_tensor(hT[:, cols(i)], hT[:, cols(i)], dsk[:, 2:3], bank[k][:],
                                               ALU.mult, ALU.add).then_inc(S["t_h"], 1)

            def center(pre):
                def body(i, k, i0):
                    dve.wait_ge(S[pre + "_mean"], i + 1)
                    nc.vector.tensor_tensor(xT[:, cols(i)], hT[:, cols(i)], bank[2 + k][:], ALU.subtract).then_inc(S[pre + "_xc"], 1)
                return body

            def scale(pre):
                def body(i, k, i0):
                    dve.wait_ge(S[pre + "_sd"], i + 1)
                    nc.vector.reciprocal(sd[k][:], sd[k][:]).then_inc(S[pre + "_rs"], 1)
                    dve.wait_ge(S[pre + "_rs"], i + 1)
                    nc.vector.tensor_tensor(xT[:, cols(i)], xT[:, cols(i)], sd[k][:], ALU.mult).then_inc(S[pre + "_xn"], 1)
                return body

            skip(0, 0, 0)
            skip(1, 1, 1)
            center("t")(0, 0, 0)

            def norm(i, k, i0):
                skip(i + 2, k, i0 + 2)
                center("t")(i + 1, 1 - k, i0 + 1)
                scale("t")(i, k, i0)
            run2(dve, NG - 2, norm)
            center("t")(NG - 1, (NG - 1) % 2, NG - 1)
            scale("t")(NG - 2, (NG - 2) % 2, NG - 2)
            scale("t")(NG - 1, (NG - 1) % 2, NG - 1)

            def gru(i, k, i0):
                for s in range(GS):
                    m = i * GS + s
                    n_ps = bank[6 + (s + k) % 2][0:HALF, 0:SEQS]
                    before = hs[k][:, s - 1, :] if s else hs[1 - k][:, GS - 1, :]
                    dve.wait_ge(S["t_rz"], m + 1)
                    dve.wait_ge(S["t_pn"], m + 1)
                    nc.vector.scalar_tensor_tensor(nt[:], rt[:], 1.0, n_ps, ALU.add, ALU.mult).then_inc(S["t_rh"], 1)
                    dve.wait_ge(S["t_rh"], m + 1)
                    nc.vector.tensor_tensor(nt[:], nt[:], gn[k][:, s, :], ALU.add).then_inc(S["t_rn"], 1)
                    wait(dve, "t_hs", m, i0 * GS + s)
                    dve.wait_ge(S["t_gz"], m + 1)
                    nc.vector.scalar_tensor_tensor(za[:], zt[:], 1.0, before, ALU.add, ALU.mult).then_inc(S["t_q"], 1)
                    dve.wait_ge(S["t_nt"], m + 1)
                    nc.vector.scalar_tensor_tensor(nb[:], zt[:], 1.0, nt[:], ALU.subtract, ALU.mult).then_inc(S["t_nb"], 1)
                    dve.wait_ge(S["t_nb"], m + 1)
                    dve.wait_ge(S["t_q"], m + 1)
                    if s == 0:
                        wait(dve, "t_hc", (i - 1) * 2, (i0 - 1) * 2)
                    nc.vector.scalar_tensor_tensor(hs[k][:, s, :], za[:], 0.5, nb[:], ALU.mult, ALU.subtract).then_inc(S["t_hs"], 1)

            run2(dve, GC, gru)
            dve.wait_ge(S["t_h4"], GC)
            skewed(dve, NG, center("t2"), scale("t2"))

            q = [GC * GS]

            def link(ins):
                ins.then_inc(S["t_q"], 1)
                q[0] += 1
                dve.wait_ge(S["t_q"], q[0])

            X = mybir.AxisListType.X
            def bc(v):
                return v[:].unsqueeze(2).broadcast_to([128, NT, E8])
            dn = down[:].unsqueeze(1).broadcast_to([128, NT, E8])
            dve.wait_ge(S["t_rt"], 1)
            nb_ = NT // 2
            for v in range(2):
                link(nc.vector.tensor_copy(lg[:, v * nb_:(v + 1) * nb_, :], bank[4 + v][:, 0:nb_ * E8].rearrange("p (t e) -> p t e", e=E8)))
            link(nc.vector.tensor_reduce(r1[:], lg[:], X, ALU.max))
            nc.vector.tensor_tensor(pr[:], lg[:], bc(r1), ALU.subtract).then_inc(S["t_lg"], 1)
            dve.wait_ge(S["t_ex"], 1)
            link(nc.vector.tensor_reduce(r2[:], pr[:], X, ALU.add))
            link(nc.vector.reciprocal(r2[:], r2[:]))
            link(nc.vector.tensor_tensor(pr[:], pr[:], bc(r2), ALU.mult))
            link(nc.vector.tensor_reduce(r1[:], pr[:], X, ALU.max))
            for v in range(2):
                src = pr if v == 0 else lg
                link(nc.vector.tensor_tensor(oh[:], src[:], bc(r1), ALU.is_equal))
                link(nc.vector.tensor_tensor(oh[:], oh[:], dn, ALU.mult))
                link(nc.vector.tensor_reduce(r3[:], oh[:], X, ALU.max))
                link(nc.vector.tensor_tensor(oh[:], oh[:], bc(r3), ALU.is_equal))
                if v == 0:
                    link(nc.vector.tensor_copy(cb[:], oh[:]))
                    link(nc.vector.tensor_copy(r2[:], r1[:]))
                    link(nc.vector.scalar_tensor_tensor(lg[:].rearrange("p t e -> p (t e)"), oh[:].rearrange("p t e -> p (t e)"), -2.0,
                                                        pr[:].rearrange("p t e -> p (t e)"), ALU.mult, ALU.add))
                    link(nc.vector.tensor_reduce(r1[:], lg[:], X, ALU.max))
            link(nc.vector.tensor_tensor(cb[:], cb[:], oh[:], ALU.add))
            link(nc.vector.tensor_tensor(cb[:], cb[:], pr[:], ALU.mult))
            link(nc.vector.tensor_tensor(r2[:], r2[:], r1[:], ALU.add))
            link(nc.vector.tensor_scalar(r2[:], r2[:], 1e-12, None, ALU.max))
            link(nc.vector.reciprocal(r2[:], r2[:]))
            link(nc.vector.tensor_tensor(cb[:], cb[:], bc(r2), ALU.mult))

            def experts(i, k, i0):
                for b in range(2):
                    for t in range(TILES):
                        n = i * (2 * TILES) + (b * TILES + t)
                        n0 = i0 * 2 * TILES + b * TILES + t
                        v = t % 2
                        dve.wait_ge(S["t_ps"], n + 1)
                        nc.vector.tensor_tensor(pd[v][:], bank[4 + v][:].rearrange("p (e d) -> p e d", e=E8),
                                                cb[:, bass.ds((i * TILES + t) * 2 + b, 1), :].rearrange("p t e -> p (t e)").unsqueeze(2).broadcast_to([128, E8, HALF]), ALU.mult).then_inc(S["t_pm"], 1)
                        dve.wait_ge(S["t_pm"], n + 1)
                        nc.vector.tensor_reduce(rd[v][:], pd[v][:].rearrange("p e d -> p d e"), X, ALU.add).then_inc(S["t_rd"], 1)
                        dve.wait_ge(S["t_rd"], n + 1)
                        if b == 0 and t == 0:
                            wait(dve, f"t_o{k}", (i - k) * 8, i0 - 1)
                        nc.vector.tensor_tensor(ob[k][:, t, 64 * b:64 * b + 64], rd[v][:], bank[6 + k][:, t * 128 + 64 * b:t * 128 + 64 * b + 64], ALU.add).then_inc(S["t_ob"], 1)
            run2(dve, NG, experts)

        @block.scalar
        def _(act):
            act.wait_ge(S["t_c"], NC_)
            act.wait_ge(S["t_z"], 6)

            def square(pre):
                def body(i, k, i0):
                    act.wait_ge(S[pre + "_xc"], i + 1)
                    wait(act, pre + "_var", i - 1, i0 - 1)
                    nc.scalar.activation(sq[k][:], xT[:, cols(i)], ACT.Square).then_inc(S[pre + "_sq"], 1)
                return body

            def root(pre):
                def body(i, k, i0):
                    act.wait_ge(S[pre + "_var"], i + 1)
                    wait(act, pre + "_xn", i - 1, i0 - 1)
                    nc.scalar.activation(sd[k][:], bank[4 + k][:], ACT.Sqrt, bias=eps[:, 0:1]).then_inc(S[pre + "_sd"], 1)
                return body

            def norm(pre):
                square(pre)(0, 0, 0)

                def both(i, k, i0):
                    root(pre)(i, k, i0)
                    square(pre)(i + 1, 1 - k, i0 + 1)
                run2(act, NG - 1, both)
                root(pre)(NG - 1, (NG - 1) % 2, NG - 1)

            act.wait_ge(S["t_c"], NC_)
            norm("t")
            act.wait_ge(S["t_w"], 6)

            def gates(i, k, i0, piece):
                if piece < 2:
                    act.wait_ge(S["t_h1"], i * 2 + (piece + 1))
                    wait(act, "t_gxm", i * 4, i0 * 4)
                    nc.scalar.activation(hg[piece][:], bank[piece][:, 0:GN], ACT.Gelu, bias=b1[:, 0:1]).then_inc(S["t_gel"], 1)
                else:
                    act.wait_ge(S["t_gxm"], i * 4 + (piece - 1))
                    wait(act, "t_rn", (i - 1) * GS, (i0 - 1) * GS)
                    b = piece % 2
                    rows, out, bias = (128, grz[k], brz) if piece < 4 else (HALF, gn[k], bn)
                    nc.scalar.activation(out[:, :, PAIRS * b:PAIRS * b + PAIRS], bank[4 + b][0:rows, 0:GN].rearrange("p (s n) -> p s n", s=GS),
                                         ACT.Identity, bias=bias[:, 0:1]).then_inc(S["t_gx"], 1)

            for piece in range(PIECES):
                gates(0, 0, 0, piece)

            def gru(i, k, i0, more=True):
                for s in range(GS):
                    m = i * GS + s
                    g_ps = bank[2 + (s + k) % 2]
                    act.wait_ge(S["t_pg"], m + 1)
                    nc.scalar.activation(rt[:], g_ps[0:HALF, 0:SEQS], ACT.Tanh, scale=0.5).then_inc(S["t_rz"], 1)
                    wait(act, "t_nb", m, i0 * GS + s)
                    nc.scalar.activation(zt[:], g_ps[HALF:128, 0:SEQS], ACT.Tanh, scale=0.5).then_inc(S["t_gz"], 1)
                    act.wait_ge(S["t_rn"], m + 1)
                    nc.scalar.activation(nt[:], nt[:], ACT.Tanh).then_inc(S["t_nt"], 1)
                    if more and s - 1 in PIECE_AT:
                        gates(i + 1, 1 - k, i0 + 1, PIECE_AT.index(s - 1))
                    if i0 > 0 and s in (2, 4):
                        state_out(i - 1, 1 - k, i0 - 1, s // 4)

            def state_out(i, k, i0, b):
                act.wait_ge(S["t_hs"], (i + 1) * GS)
                wait(act, "t_h4", i, i0)
                nc.scalar.activation(hx[HALF * b:HALF * b + HALF], hs[k][:, :, PAIRS * b:PAIRS * b + PAIRS], ACT.Copy, scale=0.5).then_inc(S["t_hc"], 1)

            run2(act, GC - 1, gru)
            gru(GC - 1, 0, GC - 1, False)
            for b in range(2):
                state_out(GC - 1, 0, GC - 1, b)

            norm("t2")
            act.wait_ge(S["t_lg"], 1)
            nc.scalar.activation(pr[:], pr[:], ACT.Exp).then_inc(S["t_ex"], 1)

            def experts(i, k, i0):
                for b in range(2):
                    for m in range(4):
                        n = i * 8 + (b * 4 + m)
                        act.wait_ge(S["t_e1"], n + 1)
                        if m == 0:
                            wait(act, "t_ps", (i * 2 + (b - 1)) * TILES, (i0 * 2 + b - 1) * TILES)
                        nc.scalar.activation(he[b][:, m, :], bank[m % 2][:], ACT.Gelu, bias=eb1[:, m:m + 1]).then_inc(S["t_eg"], 1)
            run2(act, NG, experts)

        @block.tensor
        def _(pe):
            pe.wait_ge(S["t_c"], NC_)
            pe.wait_ge(S["t_z"], 6)

            def transpose_y(i, k, i0):
                pe.wait_ge(S[f"t_y{k}"], (i - k) * 8 + (32 if i0 == NG - 1 else 16))
                wait(pe, "t_h", i - 1, i0 - 1)
                for t in range(TILES):
                    last = nc.tensor.transpose(bank[k][:, t * 128:(t + 1) * 128], yl[k][:, t, :], ident[:])
                last.then_inc(S["t_tr"], 1)

            def mean(pre, i, k, i0):
                if pre == "t":
                    pe.wait_ge(S["t_h"], i + 1)
                wait(pe, pre + "_xc", i - 1, i0 - 1)
                nc.tensor.matmul(bank[2 + k][:], ones[:], hT[:, cols(i)], start=True, stop=True).then_inc(S[pre + "_mean"], 1)

            def var(pre, i, k, i0):
                pe.wait_ge(S[pre + "_sq"], i + 1)
                wait(pe, pre + "_sd", i - 1, i0 - 1)
                nc.tensor.matmul(bank[4 + k][:], ones[:], sq[k][:], start=True, stop=True).then_inc(S[pre + "_var"], 1)

            def mean_of(pre):
                return lambda i, k, i0: mean(pre, i, k, i0)

            def var_of(pre):
                return lambda i, k, i0: var(pre, i, k, i0)

            transpose_y(0, 0, 0)
            transpose_y(1, 1, 1)

            def ahead(i, k, i0):
                mean("t", i, k, i0)
                if i0 + 2 < NG:
                    transpose_y(i + 2, k, i0 + 2)
            ahead(0, 0, 0)

            def both(i, k, i0):
                ahead(i + 1, 1 - k, i0 + 1)
                var("t", i, k, i0)
            run2(pe, NG - 4, both)
            for i in range(NG - 4, NG - 1):
                both(i, i % 2, i)
            var("t", NG - 1, (NG - 1) % 2, NG - 1)

            pe.wait_ge(S["t_w"], 6)
            pe.wait_ge(S["t_xn"], NG)
            pe.wait_ge(S["t_sd"], NG)

            def inputs(i, k, i0, piece):
                if piece < 2:
                    wait(pe, "t_gel", i * 2, i0 * 2)
                    nc.tensor.matmul(bank[piece][:, 0:GN], w1t[:, piece, :], xT[:, cols(i, GN)], start=True, stop=True).then_inc(S["t_h1"], 1)
                else:
                    if piece == 2:
                        pe.wait_ge(S["t_gel"], i * 2 + 2)
                    before = (-1, 0, 1, 2)[piece - 2]
                    wait(pe, "t_gx", i * 4 + before, i0 * 4 + before)
                    g, b = slice(0, 128) if piece < 4 else slice(128, 192), piece % 2
                    last = nc.tensor.matmul(bank[4 + b][0:128 if piece < 4 else HALF, 0:GN], wih[:, g], hg[b][:], start=True, stop=True)
                    last.then_inc(S["t_gxm"], 1)

            for piece in range(PIECES):
                inputs(0, 0, 0, piece)

            def gru(i, k, i0, more=True):
                for s in range(GS):
                    m, m0 = i * GS + s, i0 * GS + s
                    g_ps = bank[2 + (s + k) % 2][:, 0:SEQS]
                    n_ps = bank[6 + (s + k) % 2][0:HALF, 0:SEQS]
                    before = hs[k][:, s - 1, :] if s else hs[1 - k][:, GS - 1, :]
                    if s == 0:
                        pe.wait_ge(S["t_gx"], i * 4 + 4)
                    wait(pe, "t_gz", m - 1, m0 - 1)
                    wait(pe, "t_rh", m - 1, m0 - 1)
                    nc.tensor.matmul(g_ps, ident[:], grz[k][:, s, :], start=True, stop=False)
                    nc.tensor.matmul(n_ps, ident[0:HALF, 0:HALF], cn[:], start=True, stop=False)
                    wait(pe, "t_hs", m, m0)
                    nc.tensor.matmul(g_ps, whh[:, 0:128], before, start=False, stop=True).then_inc(S["t_pg"], 1)
                    nc.tensor.matmul(n_ps, whh[:, 128:192], before, start=False, stop=True).then_inc(S["t_pn"], 1)
                    if more and s in PIECE_AT:
                        inputs(i + 1, 1 - k, i0 + 1, PIECE_AT.index(s))
            run2(pe, GC - 1, gru)
            gru(GC - 1, 0, GC - 1, False)

            pe.wait_ge(S["t_h4"], GC)

            skewed(pe, NG, mean_of("t2"), var_of("t2"))

            pe.wait_ge(S["t2_xn"], NG)
            pe.wait_ge(S["t2_sd"], NG)
            for n in range(NT // 2):
                last = nc.tensor.matmul(bank[4 + n // (NT // 4)][:, n % (NT // 4) * 2 * E8:(n % (NT // 4) + 1) * 2 * E8], xT[:, n * 128:(n + 1) * 128],
                                        rw[:].rearrange("p b e -> p (b e)"), start=True, stop=True)
            last.then_inc(S["t_rt"], 1)

            def up(i, b, m, i0):
                n, n0 = i * 8 + (b * 4 + m), i0 * 8 + b * 4 + m
                wait(pe, "t_eg", n - 1, n0 - 1)
                nc.tensor.matmul(bank[m % 2][:], ew1[:, b, m, :], xT[:, cols(i)], start=True, stop=True).then_inc(S["t_e1"], 1)

            def down_one(i, k, b, j, i0):
                n, n0 = i * 8 + (b * 4 + j), i0 * 8 + b * 4 + j
                v = j % 2
                if j == 0:
                    pe.wait_ge(S["t_eg"], (i * 2 + (b + 1)) * 4)
                    pe.wait_ge(S["t_cp"], i + 1)
                wait(pe, "t_ob", n - 1, n0 - 1)
                if b == 0 and j == 0:
                    for t in range(TILES):
                        nc.tensor.transpose(bank[6 + k][:, t * 128:(t + 1) * 128], hcp[k][:, t * 128:(t + 1) * 128], ident[:])
                nc.tensor.matmul(bank[4 + v][:], one3[:], eb2r[:], start=True, stop=False)
                for m in range(4):
                    last = nc.tensor.matmul(bank[4 + v][:, m * 128:(m + 1) * 128], he[b][:, m, j * 128:(j + 1) * 128], ew2[:, m, :], start=False, stop=(m == 3))
                last.then_inc(S["t_ps"], 1)

            pe.wait_ge(S["t_br"], 16)
            for m in range(4):
                up(0, 0, m, 0)

            def experts(i, k, i0, more=True):
                for j in range(4):
                    up(i, 1, j, i0)
                    down_one(i, k, 0, j, i0)
                for j in range(4):
                    if more:
                        up(i + 1, 0, j, i0 + 1)
                    down_one(i, k, 1, j, i0)
            run2(pe, NG - 2, experts)
            experts(NG - 2, 0, NG - 2)
            experts(NG - 1, 1, NG - 1, False)


def program(nc, io):
    io["y2"] = nc.dram_tensor("y2", [CHUNKS[2] * T, PAIRS, 128], FP32, kind="Internal").ap()
    io["x2"] = nc.dram_tensor("x2", [CHUNKS[2], 128, COLS], FP32, kind="Internal").ap()
    ssm(nc, io)
    tail(nc, io)


def kernel(**inputs):
    import numpy as np
    import ml_dtypes
    import concourse.bacc as bacc
    from concourse.bass_utils import run_bass_kernel_spmd
    inp = {k: np.asarray(v) for k, v in inputs.items()}
    c0 = CHUNKS[0]
    f = np.float32

    def lay(a):
        return np.ascontiguousarray(a)

    sel = np.zeros((128, 128), ml_dtypes.bfloat16)
    for q in range(4):
        for b in range(2):
            sel[32 * q + 3 * b:32 * q + 3 * b + 3, 64 * b:64 * b + 64] = 1
    mean = np.zeros((128, 128), f)
    mean[0:64, 0:64] = mean[64:128, 64:128] = 1.0 / HALF
    arrays = {
        "xT": lay(inp["x"].reshape(2, PAIRS, c0, T, HALF).transpose(2, 0, 4, 3, 1).reshape(c0, 128, COLS)),
        "AlogT": lay(inp["L0_tok_A_log"].transpose(0, 2, 1)),
        "D": lay(inp["L0_tok_D"].T),
        "Wr": lay(inp["L0_tok_W_dbc"][:, 0, :].T),
        "WT": lay(inp["L0_tok_W_dbc"].transpose(0, 2, 1)),
        "Wdt": lay(inp["L0_tok_W_dt"][:, :, 0].T),
        "bdt": lay(inp["L0_tok_b_dt"].T),
        "sel": sel,
        "ident": np.eye(128, dtype=f),
        "W1T": lay(inp["L0_attn_W1"].T),
        "b1": lay(inp["L0_attn_b1"][:, None]),
        "WihT": lay(inp["L0_attn_W_ih"].T),
        "bih": lay(inp["L0_attn_b_ih"].reshape(3, HALF, 1)),
        "WhhT": lay(inp["L0_attn_W_hh"].T),
        "bhh": lay(inp["L0_attn_b_hh"].reshape(3, HALF, 1)),
        "ones64": mean,
        "ew1": lay(inp["L0_ffn_w1"].transpose(1, 0, 2).reshape(HALF, 4, 128)),
        "eb1": lay(inp["L0_ffn_b1"].reshape(4, 128).T),
        "ew2": lay(inp["L0_ffn_w2"].reshape(4, 2, HALF, HALF).transpose(1, 2, 0, 3)),
        "eb2": lay(inp["L0_ffn_b2"].reshape(1, 512)),
        "one3": np.ones((3, 128), ml_dtypes.bfloat16),
        "rwT": lay(inp["L0_ffn_router_w"].T),
        "down": np.tile(np.arange(8, 0, -1, dtype=f), (128, 1)),
    }
    nc = bacc.Bacc("TRN2", target_bir_lowering=False, num_devices=1)
    io = {k: nc.dram_tensor(k + "_in", a.shape, mybir.dt.from_np(a.dtype), kind="ExternalInput").ap() for k, a in arrays.items()}
    io["out"] = nc.dram_tensor("out", (TOK, 128), FP32, kind="ExternalOutput").ap()
    program(nc, io)
    r = run_bass_kernel_spmd(nc, [{k + "_in": a for k, a in arrays.items()}], core_ids=[0])
    out = r.results[0]["out"][:NTOK].reshape(SEQ[2], PAIRS, 2, HALF)
    return lay(out.transpose(2, 1, 0, 3).reshape(64, SEQ[2], HALF))
```
